# Optimizing a Trainium2 kernel written in Bass

```python
import numpy as np
import jax
import jax.numpy as jnp

def _softmax(x, axis=-1):
    return jax.nn.softmax(x, axis=axis)

def _gelu(x):
    return jax.nn.gelu(x, approximate=True)

def _silu(x):
    return jax.nn.silu(x)

def _sigmoid(x):
    return jax.nn.sigmoid(x)

def _layernorm(x, axis=-1, eps=1e-05):
    m = jnp.mean(x, axis=axis, keepdims=True)
    v = jnp.var(x, axis=axis, keepdims=True)
    return (x - m) / jnp.sqrt(v + eps)

def _scatter_add(tgt, idx, src, axis=0):
    return tgt.at[idx].add(src)

def _segment_sum(src, seg, n):
    return jax.ops.segment_sum(src, seg, n)
kernel_name = 'mk_adj_preln_d2_adj_r2_a3c699'

def setup_inputs(seed: int=0):
    np.random.seed(seed)
    _w = jnp.asarray

    def _rec_inputs():
        import jax
        import jax.numpy as jnp
        _gk = jax.random.key(seed)
        x = -0.0005207 + 1.001 * jax.random.normal(jax.random.fold_in(_gk, 1), (4096, 128), jnp.float32)
        _a = jax.random.bernoulli(jax.random.fold_in(_gk, 2), 0.000976562, (4096, 4096))
        _a = jnp.logical_or(_a, jnp.eye(4096, dtype=bool))
        _af = _a.astype(jnp.float32)
        adj = _af
        return (x, adj)
    x, adj = _rec_inputs()

    def _L0_gnn_setup():
        import jax, jax.numpy as jnp
        import numpy as np
        N = 4096
        F = 128
        NEG_INF = -9000000000000000.0
        ALPHA = 0.2
        THRESH = 1e-06
        key = jax.random.key(seed)
        k1, k2, k3, k4 = jax.random.split(key, 4)
        x = jax.random.normal(k1, (N, F), jnp.float32)
        h0 = jax.random.normal(k2, (N, F), jnp.float32)
        limit = float(np.sqrt(6.0 / (2 * F + 1)) * 1.414)
        a = jax.random.uniform(k3, (2 * F, 1), jnp.float32, -limit, limit)
        temp = jnp.zeros((5,), jnp.float32)
        adj = jax.random.bernoulli(k4, 0.005, (N, N)).astype(jnp.float32)
        adj = jnp.maximum(adj, jnp.eye(N, dtype=jnp.float32))
        return {'x': x, 'h0': h0, 'a': a, 'temp': temp, 'adj': adj, 'l': 1}
    _L0_gnn_all = _L0_gnn_setup()
    _L0_gnn_in = {k: v for k, v in _L0_gnn_all.items() if k in ('h0', 'a', 'temp')}
    del _L0_gnn_all

    def _L1_gnn_setup():
        import jax, jax.numpy as jnp
        import numpy as np
        N = 4096
        D = 128
        CUTOFF = 1.0
        MU = 1.0
        SIGMA = 0.5

        def sensitivity(r, mu, sigma):
            return jnp.exp(-(1.0 / r - 1.0 / mu) ** 2 / (2.0 * sigma * sigma))
        key = jax.random.key(seed)
        k_z, k_d, k_w = jax.random.split(key, 3)
        z = jax.random.normal(k_z, (N, D), dtype=jnp.float32)
        dist_matrix = jax.random.uniform(k_d, (N, N), dtype=jnp.float32) * 2.0 + 0.05
        W = jax.random.normal(k_w, (D, D), dtype=jnp.float32)
        B = jnp.zeros((D,), dtype=jnp.float32)
        return {'z': z, 'dist_matrix': dist_matrix, 'W': W, 'B': B}
    _L1_gnn_all = _L1_gnn_setup()
    _L1_gnn_in = {k: v for k, v in _L1_gnn_all.items() if k in ('W', 'B')}
    del _L1_gnn_all
    return {'x': x, 'adj': adj, 'L0_gnn_h0': _L0_gnn_in['h0'], 'L0_gnn_a': _L0_gnn_in['a'], 'L0_gnn_temp': _L0_gnn_in['temp'], 'L1_gnn_W': _L1_gnn_in['W'], 'L1_gnn_B': _L1_gnn_in['B']}

def reference(x, adj, L0_gnn_h0, L0_gnn_a, L0_gnn_temp, L1_gnn_W, L1_gnn_B):
    import jax
    import jax.numpy as jnp

    def _L0_gnn_ref(x, h0, a, temp, adj, l):
        import jax, jax.numpy as jnp
        import numpy as np
        N = 4096
        F = 128
        NEG_INF = -9000000000000000.0
        ALPHA = 0.2
        THRESH = 1e-06
        Fdim = x.shape[1]
        feat_1 = x @ a[:Fdim]
        feat_2 = x @ a[Fdim:]
        e = jax.nn.leaky_relu(feat_1 + feat_2.T, ALPHA)
        att = jnp.where(adj > 0, e, NEG_INF)
        U = jax.nn.softmax(att, axis=1)
        P = 0.5 * U
        prop_u = U @ x
        rowsum = jnp.sum(U * P, axis=1)
        coe = jax.nn.sigmoid(temp)
        xi = x * rowsum[:, None]
        feat_odd = prop_u - xi
        feat_even = x + prop_u - xi
        feat = coe[2] * feat_odd + (1.0 - coe[2]) * feat_even
        sgn = jnp.sign(feat)
        mod = jnp.abs(feat)
        mod = jnp.where(mod > THRESH, mod - THRESH, 0.0)
        feat = mod * sgn
        pu = U @ feat
        feat_odd2 = feat - coe[3] * pu
        feat_even2 = pu + feat_odd2 * rowsum[:, None]
        feat_odd2 = coe[0] * feat_odd2 + (1.0 - coe[0]) * h0
        out = coe[1] * feat_even2 + (1.0 - coe[1]) * feat_odd2
        return out

    def _L1_gnn_ref(z, dist_matrix, W, B):
        import jax, jax.numpy as jnp
        import numpy as np
        N = 4096
        D = 128
        CUTOFF = 1.0
        MU = 1.0
        SIGMA = 0.5

        def sensitivity(r, mu, sigma):
            return jnp.exp(-(1.0 / r - 1.0 / mu) ** 2 / (2.0 * sigma * sigma))
        msg = z @ W + B
        sens = sensitivity(dist_matrix, MU, SIGMA)
        weights = jnp.where(dist_matrix < CUTOFF, sens, 0.0)
        return weights @ msg
    h = jnp.maximum(_layernorm(x, axis=-1), 0.0)
    x = x + _L0_gnn_ref(h, L0_gnn_h0, L0_gnn_a, L0_gnn_temp, adj, 1)
    h = jnp.maximum(_layernorm(x, axis=-1), 0.0)
    x = x + _L1_gnn_ref(h, adj, L1_gnn_W, L1_gnn_B)
    return x

_drawn_inputs = setup_inputs


def setup_inputs(seed=0):
    import zlib

    import numpy as np

    out = dict(_drawn_inputs(seed))
    spreads = {'L0_gnn_temp': (0.0, 0.8), 'L1_gnn_B': (0.0, 0.1)}
    factors = {}
    for name, (base, spread) in spreads.items():
        noise = np.random.default_rng([zlib.crc32(name.encode()), seed]).standard_normal(out[name].shape)
        drawn = base * np.exp(spread * noise) if base else spread * noise
        out[name] = jnp.asarray(drawn.astype(out[name].dtype))
    for name, factor in factors.items():
        out[name] = (out[name] * factor).astype(out[name].dtype)
    return out
```

```python
import concourse.bass as bass
from concourse import mybir
from contextlib import ExitStack
import numpy as np

FP32, FP16, FP8 = mybir.dt.float32, mybir.dt.float16, mybir.dt.float8e4
U8, I8, I32, U32 = mybir.dt.uint8, mybir.dt.int8, mybir.dt.int32, mybir.dt.uint32
ALU, ACT, AX = mybir.AluOpType, mybir.ActivationFunctionType, mybir.AxisListType

P = 128
N, F = 4096, 128
T = N // P
PAIRS = T // 2
QUAD = 4
LANE = P // QUAD
JQ = N // QUAD
NB = JQ // P
E4 = 4
SLOPE, EPS, THRESH, NEG_INF = 0.2, 1e-5, 1e-6, -9e15
F2_RANGE = 10.0

S_H = 4096.0
S_SQ = 32768.0
S_F = 2048.0
W1 = 262
LO = 130
CNT = 260
W2 = 256

POS = (0x40, 0x10)
NEG = (0x20, 0x08)
POS_VAL = (2.0, 2.0 ** -5)
NEG_VAL = (2.0 ** -3, 2.0 ** -6)


RING = 4
STEPS1 = 15
STEPS2 = 6


def word(byte):
    return int(byte) * 0x01010101


def build(nc, x, adj, h0, a, temp, w_msg, b_msg, out):
    feat_scratch = nc.dram_tensor("feat_scratch", (PAIRS, P, 2 * F), FP32).ap()
    ctx = ExitStack()
    with ctx:
        def sb(name, shape, dt):
            return ctx.enter_context(nc.sbuf_tensor(name, shape, dt))

        def sem(name):
            return ctx.enter_context(nc.semaphore(name))

        codes = sb("codes", [P, PAIRS, NB, P], I32)
        xb = sb("xb", [P, T, W1], FP16)
        xd = sb("xd", [P, T, W1], FP16)
        fb = sb("fb", [P, T, W2], FP16)
        fd = sb("fd", [P, T, W2], FP16)
        adj_ring = sb("adj_ring", [P, 4, 2 * JQ], FP32)
        edge = sb("edge", [P, 2, N], U8)
        side = sb("side", [P, 2, N], I8)
        both_t = sb("both_t", [P, NB, P], I32)
        flags = sb("flags", [P, RING, 4, P], I32)
        f2_all = sb("f2_all", [P, JQ], FP32)
        f1_rep = sb("f1_rep", [P, QUAD, T], FP32)
        nz = sb("nz", [P, 2 * T], FP32)
        cnt = sb("cnt", [P, T, 2], FP32)
        ac = sb("ac", [P, 2, T], FP32)
        ac1 = sb("ac1", [P, 2, T], FP32)
        ac2 = sb("ac2", [P, 2, T], FP32)
        rden = sb("rden", [P, T], FP32)
        rs = sb("rs", [P, T], FP32)
        wmix = sb("wmix", [P, T], FP32)
        bd = sb("bd", [P, 2, T], FP32)
        bdh = sb("bdh", [P, 2, T], FP32)
        bdf = sb("bdf", [P, 2, T], FP32)
        rstd = sb("rstd", [P, T], FP32)
        nmr = sb("nmr", [P, T], FP32)
        coe = sb("coe", [P, 5], FP32)
        cmix = sb("cmix", [P, 6], FP32)
        small = sb("small", [P, 5, 4], FP32)
        acsq = sb("acsq", [P, 2, T], FP32)
        ones_col = sb("ones_col", [P, 1], FP32)
        wrong = sb("wrong", [P, 4], FP32)
        rows_n = sb("rows_n", [P, T], FP32)
        flag_i = sb("flag_i", [1, 1], I32)
        rows = sb("rows", [P, 2, 2, F], FP32)
        ev = sb("ev", [P, 2, 2, W1], FP32)
        acc = sb("acc", [P, 2, LO * 2], FP32)
        num = sb("num", [P, 2, F + 1], FP32)
        feat = sb("feat", [P, 2, 2, F], FP32)
        print("SBUF left", nc.sbuf_bytes_remaining if not callable(nc.sbuf_bytes_remaining) else nc.sbuf_bytes_remaining())

        early = codes[:, PAIRS // 2:, :, :].bitcast(FP32).rearrange("p s b i -> p (s b i)")
        x_all = early[:, 0:T * F].rearrange("p (t f) -> p t f", f=F)
        h_all = early[:, T * F:2 * T * F].rearrange("p (t f) -> p t f", f=F)
        scrap = fb[:, :, :].rearrange("p t w -> p (t w)").bitcast(FP32)
        h_t = scrap[:, 0:1024].rearrange("p (s w) -> p s w", s=2)
        spread = scrap[:, 1024:2048]
        scaled = scrap[:, 2048:4096].rearrange("p (s w) -> p s w", s=4)
        scrap2 = fd[:, :, :].rearrange("p t w -> p (t w)").bitcast(FP32)
        ident = scrap2[:, 0:128]
        quads = scrap2[:, 128:256]
        lanes = scrap2[:, 256:384].rearrange("p (a c) -> p a c", a=QUAD)
        ones = scrap2[:, 384:512]
        f1_spread = scrap2[:, 512:640].rearrange("p (g t) -> p g t", g=QUAD)
        stats = scrap2[:, 640:640 + 6 * T].rearrange("p (t s) -> p t s", s=6)
        mv = scrap2[:, 1024:1024 + 2 * T].rearrange("p (t s) -> p t s", s=2)
        a12 = scrap2[:, 1100:1102]
        fj = scrap2[:, 1104:1104 + 2 * T].rearrange("p (k t) -> p k t", k=2)
        tmp = scrap2[:, 1200:1200 + 8 * T].rearrange("p (n t) -> p n t", t=T)
        ext = scrap2[:, 1500:1540]

        g_rows = codes[:, :, :, :].bitcast(FP32).rearrange("p s b i -> p (s b i)")
        g_f2, g_x, g_h0, g_msg = (g_rows[:, N * n:N * (n + 1)] for n in range(4))
        g_x, g_h0, g_msg = (w.rearrange("p (t f) -> p t f", f=F) for w in (g_x, g_h0, g_msg))
        g_h = scrap.rearrange("p (t f) -> p t f", f=F)
        g_feat = scrap2.rearrange("p (t f) -> p t f", f=F)
        g_adj = adj_ring[:, 0:2, :].rearrange("p s j -> p (s j)")
        g_w = xb[:, :, :].rearrange("p t w -> p (t w)").bitcast(FP32)[:, 0:N]
        g_t = xd[:, :, :].rearrange("p t w -> p (t w)").bitcast(FP32)[:, 0:N]
        g_more = adj_ring[:, 2:4, :].rearrange("p s j -> p (s j)")
        g_wt, g_ident, g_wm, g_bm, g_a2, g_ht = (g_more[:, 512 * n:512 * n + w] for n, w in
                                                 enumerate((512, P, F, F, P, 512)))
        g_st = g_more[:, 3072:3072 + 6 * T].rearrange("p (t s) -> p t s", s=6)
        g_mv = g_more[:, 3328:3328 + 2 * T].rearrange("p (t s) -> p t s", s=2)
        g_tmp = g_more[:, 3400:3400 + 5 * T].rearrange("p (n t) -> p n t", t=T)
        g_f1 = g_more[:, 3600:3600 + T]
        g_rs = g_more[:, 3640:3640 + T]
        g_a12 = g_more[:, 3680:3682]
        g_s = g_more[:, 3700:3712]

        ps = ctx.enter_context(nc.psum_tensor("ps", [P, 2, 2, 512], FP32))
        ps_t = ctx.enter_context(nc.psum_tensor("ps_t", [P, 2, 512], FP32))
        ps_f = ctx.enter_context(nc.psum_tensor("ps_f", [P, 512], FP32))
        ps_s = ctx.enter_context(nc.psum_tensor("ps_s", [P, 512], FP32))

        x_in = [sem(f"x_in{c}") for c in range(NB)]
        a_in = sem("a_in")
        adj_in = [sem(f"adj_in{s}") for s in range(4)]
        row_in = [sem(f"row_in{s}") for s in range(2)]
        aux_in = [sem(f"aux_in{s}") for s in range(2)]
        feat_out = [sem(f"feat_out{s}") for s in range(2)]
        out_done = [sem(f"out_done{s}") for s in range(2)]
        const_ok = sem("const_ok")
        v = sem("v")
        var_ok = sem("var_ok")
        root_ok = sem("root_ok")
        xn_ok = sem("xn_ok")
        h_chunk_ok = sem("h_chunk_ok")
        turned_ok = sem("turned_ok")
        h_t_ok = sem("h_t_ok")
        f_ok = sem("f_ok")
        spread_ok = sem("spread_ok")
        f2_ps_ok = sem("f2_ps_ok")
        f2_ok = sem("f2_ok")
        f1_ok = sem("f1_ok")
        ext_ok = sem("ext_ok")
        ext_ps_ok = sem("ext_ps_ok")
        arg_ok = sem("arg_ok")
        exp_ok = sem("exp_ok")
        temp_ok = sem("temp_ok")
        scaled_ok = sem("scaled_ok")
        high_ok = sem("high_ok")
        low_ok = sem("low_ok")
        ready_ok = sem("ready_ok")
        edge_ok = sem("edge_ok")
        count_ok = sem("count_ok")
        side_ok = sem("side_ok")
        side_used = sem("side_used")
        merged = sem("merged")
        both_ok = sem("both_ok")
        saved = sem("saved")
        flags_ok = sem("flags_ok")
        turn = sem("turn")
        flags_used = sem("flags_used")
        sums_used = sem("sums_used")
        ev_used = sem("ev_used")
        h_ok = sem("h_ok")
        row_used = sem("row_used")
        step1 = sem("step1")
        feat_ok = sem("feat_ok")
        feat_free = sem("feat_free")
        hi_ok = sem("hi_ok")
        feats_ok = sem("feats_ok")
        step2 = sem("step2")
        y_ok = sem("y_ok")
        wrong_ok = sem("wrong_ok")
        wrong_ps_ok = sem("wrong_ps_ok")
        flag_ok = sem("flag_ok")
        g_in = sem("g_in")
        g_adj_in = sem("g_adj_in")
        g_const = sem("g_const")
        g_seen = sem("g_seen")
        g_root = sem("g_root")
        g_var = sem("g_var")
        g_hn = sem("g_hn")
        g_turned = sem("g_turned")
        g_t_ok = sem("g_t_ok")
        g_f = sem("g_f")
        g_scored = sem("g_scored")
        g_exp = sem("g_exp")
        g_w_ok = sem("g_w_ok")
        g_sq = sem("g_sq")
        g_wt_ps = sem("g_wt_ps")
        g_wt_ok = sem("g_wt_ok")
        g_prod = sem("g_prod")
        g_done = sem("g_done")
        g_out = sem("g_out")
        block = ctx.enter_context(nc.Block())

        def after(eng, sem_, value):
            eng.wait_ge(sem_, value)
            eng.sem_inc(g_seen, 1)

        def general(eng):
            eng.wait_ge(flag_ok, 1)
            return eng.If(eng.value_load(flag_i[0:1, 0:1], min_val=0, max_val=1) == 1)

        adj_v = adj.rearrange("(g b c e) (a j) -> a b e c g j", g=QUAD, b=NB, c=LANE, e=E4, a=QUAD)
        x_v = x.rearrange("(g b c e) f -> g b c (e f)", g=QUAD, b=NB, c=LANE, e=E4)
        h0_v = h0.rearrange("(g b c e) f -> g b c (e f)", g=QUAD, b=NB, c=LANE, e=E4)
        out_v = out.rearrange("(g b c e) f -> g b c (e f)", g=QUAD, b=NB, c=LANE, e=E4)

        aux = adj_ring[:, :, :].rearrange("p s j -> p (s j)")
        h0_rows, x_rows, feat_rows, y_rows = (
            aux[:, 512 * n:512 * (n + 1)].rearrange("p (s e f) -> p s e f", s=2, e=2) for n in range(4))

        def pair_rows(view, b, h, g):
            return view[g, b, :, 2 * F * h:2 * F * (h + 1)]

        def lanes_of(tile, g):
            return tile[LANE * g:LANE * (g + 1)].rearrange("c e f -> c (e f)")

        @block.sync
        def _(sp):
            def load_adj(b, e, half, slot):
                for q in range(QUAD):
                    sp.dma_start(adj_ring[LANE * q:LANE * (q + 1), slot, :].rearrange("c (g j) -> c g j", g=2),
                                 adj_v[q, b, e, :, 2 * half:2 * half + 2, :]).then_inc(adj_in[slot], 16)

            def slot_free(n):
                sp.wait_ge(edge_ok, n + 1)
                sp.wait_ge(count_ok, n + 1)

            for b in range(NB):
                for g in range(QUAD):
                    sp.dma_start(lanes_of(x_all[:, E4 * b:E4 * (b + 1), :], g), x_v[g, b]).then_inc(x_in[b], 16)
            for u in range(4):
                load_adj(0, u // 2, u % 2, u)
            with sp.Fori(0, NB - 1) as b:
                for k in range(8):
                    slot_free(8 * b + k)
                    load_adj(b + (4 + k) // 8, (4 + k) % 8 // 2, k % 2, k % 4)
            for k in range(4):
                slot_free(8 * (NB - 1) + k)
                load_adj(NB - 1, 2 + k // 2, k % 2, k)

            def load_aux(b, h):
                for g in range(QUAD):
                    sp.dma_start(lanes_of(h0_rows[:, h], g), pair_rows(h0_v, b, h, g)).then_inc(aux_in[h], 16)
                    sp.dma_start(lanes_of(x_rows[:, h], g), pair_rows(x_v, b, h, g)).then_inc(aux_in[h], 16)
                sp.dma_start(feat_rows[:, h].rearrange("p e f -> p (e f)"),
                             feat_scratch[bass.ds(2 * b + h, 1)].rearrange("o p w -> (o p) w")).then_inc(aux_in[h], 16)

            def store_out(b, h):
                sp.wait_ge(y_ok, 2 * b + h + 1)
                for g in range(QUAD):
                    sp.dma_start(pair_rows(out_v, b, h, g), lanes_of(y_rows[:, h], g)).then_inc(out_done[h], 16)

            slot_free(2 * T - 1)
            for s in range(2):
                sp.wait_ge(feat_out[s], 16 * PAIRS // 2)
            load_aux(0, 0)
            load_aux(0, 1)
            with sp.Fori(0, NB - 1) as b:
                for h in range(2):
                    store_out(b, h)
                    load_aux(b + 1, h)
            for h in range(2):
                store_out(NB - 1, h)
            for s in range(2):
                sp.wait_ge(out_done[s], 64 * (NB + 1))

            with general(sp):
                rows_of = lambda m: m.rearrange("(t p) f -> p t f", p=P)
                sp.dma_start(g_x, rows_of(x)).then_inc(g_in, 16)
                sp.dma_start(g_h0, rows_of(h0)).then_inc(g_in, 16)
                sp.dma_start(g_wm, w_msg).then_inc(g_in, 16)
                sp.dma_start(g_bm, b_msg.rearrange("(o f) -> o f", o=1).broadcast_to([P, F])).then_inc(g_in, 16)
                sp.dma_start(g_a12, a.rearrange("(k f) o -> f (k o)", k=2), allow_slow_non_contiguous=True)\
                    .then_inc(g_in, 16)
                adj_rows = adj.rearrange("(t p) j -> t p j", p=P)
                for phase in range(3):
                    if phase:
                        sp.wait_ge(g_w_ok, T * phase)
                    sp.dma_start(g_adj, adj_rows[0]).then_inc(g_adj_in, 16)
                    with sp.Fori(0, T - 1) as t:
                        sp.wait_ge(g_w_ok, T * phase + t + 1)
                        sp.dma_start(g_adj, adj_rows[bass.ds(t + 1, 1)].rearrange("o p j -> (o p) j")).then_inc(g_adj_in, 16)
                sp.wait_ge(g_done, 1)
                sp.dma_start(rows_of(out), g_x).then_inc(g_out, 16)
                sp.wait_ge(g_out, 16)

        @block.gpsimd
        def _(pool):
            pool.memset(ident, 0.0).then_inc(const_ok, 1)
            pool.memset(quads, 0.0).then_inc(const_ok, 1)
            pool.memset(ones, 1.0).then_inc(const_ok, 1)
            pool.wait_ge(const_ok, 3)
            pool.affine_select(out=ident, in_=ident, compare_op=ALU.not_equal, fill=1.0, base=0,
                               pattern=[[-1, P]], channel_multiplier=1).then_inc(const_ok, 1)
            for q in range(QUAD):
                pool.wait_ge(const_ok, 4 + q)
                pool.memset(quads[LANE * q:LANE * (q + 1), LANE * q:LANE * (q + 1)], 1.0).then_inc(const_ok, 1)

            def load_rows(b, h):
                for g in range(QUAD):
                    pool.dma_start(lanes_of(rows[:, h], g), pair_rows(x_v, b, h, g)).then_inc(row_in[h], 16)

            def save(p):
                pool.wait_ge(both_ok, p + 1)
                pool.tensor_copy(codes[:, bass.ds(p, 1), :, :], both_t[:, None, :, :]).then_inc(saved, 1)

            def store_feat(b, h):
                pool.wait_ge(feat_ok, 2 * b + h + 1)
                pool.dma_start(feat_scratch[bass.ds(2 * b + h, 1)].rearrange("o p w -> (o p) w"),
                               feat[:, h].rearrange("p e f -> p (e f)")).then_inc(feat_out[h], 16)

            load_rows(0, 0)
            load_rows(0, 1)
            save(0)
            with pool.Fori(0, NB - 1) as b:
                for h in range(2):
                    save(2 * b + h + 1)
                    store_feat(b, h)
                    pool.wait_ge(row_used, 2 * b + h + 1)
                    load_rows(b + 1, h)
                    pool.wait_ge(feat_out[h], 16 * (b + 1))
                    pool.sem_inc(feat_free, 1)
            save(PAIRS - 1)
            for h in range(2):
                store_feat(NB - 1, h)
            for h in range(2):
                pool.wait_ge(feat_out[h], 16 * PAIRS // 2)

            with general(pool):
                pool.memset(g_ident, 0.0).then_inc(g_const, 1)
                pool.wait_ge(g_const, 1)
                pool.affine_select(out=g_ident, in_=g_ident, compare_op=ALU.not_equal, fill=1.0, base=0,
                                   pattern=[[-1, P]], channel_multiplier=1).then_inc(g_const, 1)

        @block.scalar
        def _(act):
            act.dma_start(a12, a.rearrange("(k f) o -> f (k o)", k=2), allow_slow_non_contiguous=True).then_inc(a_in, 16)
            act.dma_start(coe[:, :], temp.rearrange("(o k) -> o k", o=1).broadcast_to([P, 5])).then_inc(a_in, 16)
            act.wait_ge(var_ok, 1)
            act.activation(tmp[:, 1], tmp[:, 0], ACT.Sqrt).then_inc(root_ok, 1)
            for b in range(NB):
                act.wait_ge(xn_ok, b + 1)
                act.activation(h_all[:, E4 * b:E4 * (b + 1), :], x_all[:, E4 * b:E4 * (b + 1), :],
                               ACT.Relu).then_inc(h_chunk_ok, 1)
            act.wait_ge(a_in, 32)
            act.activation(coe[:, :], coe[:, :], ACT.Exp, scale=-1.0).then_inc(temp_ok, 1)
            for n in range(2):
                act.wait_ge(f2_ps_ok, n + 1)
                act.activation(f2_all[:, 512 * n:512 * (n + 1)], ps_t[:, n], ACT.Copy).then_inc(f2_ok, 1)
            act.wait_ge(arg_ok, 4)
            act.activation(bd[:, :, :], tmp[:, 2:4], ACT.Exp).then_inc(exp_ok, 1)
            act.activation(ac[:, :, :], tmp[:, 4:6], ACT.Exp).then_inc(exp_ok, 1)
            for b in range(NB):
                for k, dst in enumerate((xb, xd)):
                    act.wait_ge(scaled_ok, 2 * b + k + 1)
                    act.activation(dst[:, E4 * b:E4 * (b + 1), 0:F],
                                   scaled[:, 2 * (b % 2) + k].rearrange("p (e f) -> p e f", e=E4),
                                   ACT.Copy).then_inc(high_ok, 1)

            def count(p, q, half):
                n = 2 * q + half
                act.wait_ge(adj_in[n], 64 * (p + 1))
                act.wait_ge(side_used, 2 * p + q + 1)
                act.activation(side[:, q, 2 * JQ * half:2 * JQ * (half + 1)], adj_ring[:, n, :].bitcast(U32), ACT.Sign,
                               accum_out=nz[:, bass.ds(4 * p + n, 1)]).then_inc(count_ok, 1)

            def compare(p, q):
                act.wait_ge(count_ok, 4 * p + 2 * q + 2)
                for g in range(QUAD):
                    last = act.activation(side[:, q, JQ * g:JQ * (g + 1)], f2_all[:, :], ACT.Sign,
                                          bias=f1_rep[:, g, bass.ds(2 * p + q, 1)])
                last.then_inc(side_ok, 1)

            def drain(p, q, width):
                act.wait_ge(flags_used, 4 * (2 * p + q + 1) + RING)
                act.wait_ge(ev_used, p + 1)
                act.activation(ev[:, q, :, 0:width], ps[:, q, :, 0:width], ACT.Copy).then_inc(sums_used, 1)

            def h_again(i, h):
                act.wait_ge(row_in[h], 64 * (i + 1))
                for q in range(2):
                    t = bass.ds(4 * i + 2 * h + q, 1)
                    last = act.activation(rows[:, h, q, :], rows[:, h, q, :], ACT.Relu, scale=rstd[:, t], bias=nmr[:, t])
                last.then_inc(h_ok, 1)

            def high(i, h):
                act.wait_ge(feat_ok, 2 * i + h + 1)
                for q in range(2):
                    t = bass.ds(4 * i + 2 * h + q, 1)
                    for k, dst in enumerate((fb, fd)):
                        last = act.activation(dst[:, t, 0:F], feat[:, h, q:q + 1, :], ACT.Copy, scale=bdf[:, k, t])
                last.then_inc(hi_ok, 1)

            def front(p, i=None, h=None):
                for q in range(2):
                    count(p, q, 0)
                    count(p, q, 1)
                    compare(p, q)
                    if i is not None:
                        if q == 0:
                            h_again(i, h)
                        drain(2 * i + h, q, W1)
                if i is not None:
                    high(i, h)

            act.wait_ge(f1_ok, 1)
            front(0)
            with act.Fori(0, NB - 1) as i:
                front(2 * i + 1, i, 0)
                front(2 * i + 2, i, 1)
            front(PAIRS - 1, NB - 1, 0)
            h_again(NB - 1, 1)
            for q in range(2):
                drain(PAIRS - 1, q, W1)
            high(NB - 1, 1)
            with act.Fori(PAIRS, 2 * PAIRS) as p:
                for q in range(2):
                    drain(p, q, W2)

            with general(act):
                act.wait_ge(g_var, 1)
                act.activation(g_tmp[:, 1], g_tmp[:, 0], ACT.Sqrt).then_inc(g_root, 1)
                for phase in range(3):
                    with act.Fori(0, T) as t:
                        n = T * phase + t
                        after(act, g_scored, n + 1)
                        if phase < 2:
                            act.activation(g_w, g_w, ACT.Exp, bias=g_s[:, 1:2], accum_out=g_s[:, 2:3]).then_inc(g_exp, 1)
                            after(act, g_w_ok, n + 1)
                            act.activation(g_t, g_w, ACT.Square, accum_out=g_s[:, 4:5]).then_inc(g_sq, 1)
                        else:
                            act.activation(g_t, g_w, ACT.Square, bias=g_s[:, 5:6]).then_inc(g_sq, 1)
                            after(act, g_sq, n + 1)
                            act.activation(g_w, g_t, ACT.Exp, scale=-2.0).then_inc(g_exp, 1)
                        if phase == 1:
                            after(act, g_var, t + 2)
                            act.activation(g_s[:, 7:8], g_s[:, 6:7], ACT.Sqrt).then_inc(g_root, 1)

        @block.tensor
        def _(pe):
            pe.sem_inc(flags_used, RING)
            pe.wait_ge(const_ok, 8)
            pe.wait_ge(a_in, 32)

            def project(b):
                pe.wait_ge(h_t_ok, b + 1)
                for e in range(E4):
                    last = pe.matmul(ps_f[:, 2 * (E4 * b + e):2 * (E4 * b + e) + 2], h_t[:, b % 2, P * e:P * (e + 1)], a12,
                                     start=True, stop=True)
                last.then_inc(f_ok, 1)

            for b in range(NB):
                pe.wait_ge(h_chunk_ok, b + 1)
                if b >= 2:
                    pe.wait_ge(h_t_ok, b - 1)
                for e in range(E4):
                    last = pe.transpose(ps_t[:, b % 2, P * e:P * (e + 1)], h_all[:, E4 * b + e, :], ident)
                last.then_inc(turned_ok, 1)
                if b >= 1:
                    project(b - 1)
            project(NB - 1)
            pe.wait_ge(spread_ok, 2)
            for n in range(2):
                pe.matmul(ps_t[:, n], quads, spread[:, 512 * n:512 * (n + 1)], start=True, stop=True).then_inc(f2_ps_ok, 1)
            pe.matmul(ps_s[:, 0:P], lanes.rearrange("p a c -> p (a c)"), f1_spread.rearrange("p g t -> p (g t)"),
                      start=True, stop=True).then_inc(f2_ps_ok, 1)
            pe.wait_ge(ext_ok, 1)
            pe.matmul(ps_f[:, P:P + 8], ones, ext[:, 2:10], start=True, stop=True).then_inc(ext_ps_ok, 1)

            def tile_sums(p, q, ops, width, gate):
                pe.wait_ge(sums_used, 2 * p + q + 1)
                for half in range(2):
                    for k in range(2):
                        s = 4 * q + 2 * half + k
                        pe.wait_ge(flags_ok, 8 * p + s + 1)
                        pe.sem_inc(turn, 1)
                        bytes_ = flags[:, s % RING].bitcast(FP8).rearrange("p b (i e) -> p b i e", e=E4)
                        for b in range(4):
                            for e in range(E4):
                                t = E4 * (4 * half + b) + e
                                if k == 0 and gate is not None:
                                    gate(t)
                                last = pe.matmul(ps[:, q, k, 0:width], bytes_[:, b, :, e], ops[k][:, t, 0:width],
                                                 start=(t == 0), stop=(t == T - 1))
                        last.then_inc(flags_used, 1)

            pe.wait_ge(low_ok, NB)
            pe.wait_ge(ready_ok, 1)
            with pe.Fori(0, PAIRS) as p:
                for q in range(2):
                    tile_sums(p, q, (xb, xd), W1, None)

            def feats_there(t):
                if t % 8 == 0 or t == T - 2:
                    pe.wait_ge(feats_ok, min(t // 2 + 4, PAIRS - 1) if t < T - 2 else PAIRS)

            with pe.Fori(PAIRS, 2 * PAIRS) as p:
                for q in range(2):
                    tile_sums(p, q, (fb, fd), W2, feats_there if q == 0 else None)
            pe.wait_ge(wrong_ok, 1)
            pe.matmul(ps_s[0:1, 0:1], wrong[:, 3:4], ones_col[:, :], start=True, stop=True).then_inc(wrong_ps_ok, 1)

            with general(pe):
                pe.wait_ge(g_const, 2)
                for b in range(NB):
                    if b == 0:
                        pe.wait_ge(g_hn, 1)
                    for e in range(E4):
                        last = pe.transpose(ps_t[:, 0, P * e:P * (e + 1)], g_h[:, E4 * b + e, :], g_ident)
                    last.then_inc(g_turned, 1)
                    pe.wait_ge(g_t_ok, b + 1)
                    for e in range(E4):
                        pe.matmul(ps_f[:, E4 * b + e:E4 * b + e + 1], g_ht[:, P * e:P * (e + 1)], g_a12[:, 0:1],
                                  start=True, stop=True)
                    pe.matmul(ps_t[:, 1], g_a2, g_ht, start=True, stop=True).then_inc(g_f, 1)
                for phase, rhs in enumerate((g_h, g_feat, g_msg)):
                    with pe.Fori(0, T) as t:
                        n = T * phase + t
                        after(pe, g_w_ok, n + 1)
                        for k in range(8):
                            for c in range(4):
                                last = pe.transpose(ps_t[:, 0, P * c:P * (c + 1)], g_w[:, P * (4 * k + c):P * (4 * k + c + 1)],
                                                    g_ident)
                            last.then_inc(g_wt_ps, 1)
                            after(pe, g_wt_ok, 8 * n + k + 1)
                            for c in range(4):
                                last = pe.matmul(ps_s[:, 0:F], g_wt[:, P * c:P * (c + 1)], rhs[:, 4 * k + c, :],
                                                 start=(k == 0 and c == 0), stop=(k == 7 and c == 3))
                            last.then_inc(g_prod, 1)
                        if phase == 1:
                            after(pe, g_hn, t + 2)
                            pe.transpose(ps_f[:, 0:P], g_ht[:, 0:P], g_ident).then_inc(g_turned, 1)
                            after(pe, g_t_ok, NB + t + 1)
                            pe.matmul(ps_t[:, 1, 0:F], g_ht[:, P:2 * P], g_wm, start=True, stop=True).then_inc(g_f, 1)

        @block.vector
        def _(dve):
            links = [0]

            def chain(ins):
                links[0] += 1
                ins.then_inc(v, 1)
                dve.wait_ge(v, links[0])

            dve.sem_inc(ev_used, 1)
            dve.sem_inc(side_used, 2)
            dve.sem_inc(sums_used, 2)
            dve.sem_inc(feat_free, 2)
            for h in range(2):
                dve.sem_inc(out_done[h], 64)
            dve.memset(ones_col[:, :], 1.0)
            for b in range(NB):
                dve.wait_ge(x_in[b], 64)
                for t in range(E4 * b, E4 * (b + 1)):
                    ins = dve.bn_stats(stats[:, t, :], x_all[:, t, :])
                chain(ins)
                for t in range(E4 * b, E4 * (b + 1)):
                    ins = dve.bn_aggr(mv[:, t, :], stats[:, t, :])
            chain(ins)
            dve.tensor_scalar(tmp[:, 0], mv[:, :, 1], EPS, None, ALU.add).then_inc(var_ok, 1)
            dve.wait_ge(root_ok, 1)
            chain(dve.reciprocal(tmp[:, 2], tmp[:, 1]))
            chain(dve.tensor_tensor(tmp[:, 3], tmp[:, 0], tmp[:, 2], ALU.mult))
            chain(dve.tensor_tensor(tmp[:, 4], tmp[:, 1], tmp[:, 3], ALU.add))
            chain(dve.tensor_scalar(tmp[:, 5], tmp[:, 4], 0.5, None, ALU.mult))
            chain(dve.reciprocal(rstd[:, :], tmp[:, 5]))
            chain(dve.scalar_tensor_tensor(out=nmr[:, :], in0=mv[:, :, 0], scalar=-1.0, in1=rstd[:, :],
                                           op0=ALU.mult, op1=ALU.mult))
            for b in range(NB):
                for t in range(E4 * b, E4 * (b + 1)):
                    ins = dve.tensor_scalar(x_all[:, t, :], x_all[:, t, :], rstd[:, t:t + 1], nmr[:, t:t + 1],
                                            ALU.mult, ALU.add)
                ins.then_inc(xn_ok, 1)
            dve.wait_ge(const_ok, 8)
            for q in range(QUAD):
                ins = dve.tensor_reduce(lanes[:, q, :], ident.rearrange("p (a c) -> p c a", a=QUAD), AX.X, ALU.add)
            chain(ins)
            for b in range(NB):
                dve.wait_ge(turned_ok, b + 1)
                if b >= 2:
                    dve.wait_ge(f_ok, b - 1)
                dve.tensor_copy(h_t[:, b % 2], ps_t[:, b % 2]).then_inc(h_t_ok, 1)
            dve.wait_ge(f_ok, NB)
            chain(dve.tensor_copy(fj, ps_f[:, 0:2 * T].rearrange("p (t k) -> p k t", k=2)))
            dve.tensor_tensor(spread.rearrange("p (b r e) -> p b r e", b=NB, e=E4),
                              fj[:, 1, :].rearrange("p (b e) -> p b e", e=E4)[:, :, None, :].broadcast_to([P, NB, LANE, E4]),
                              lanes[:, 0, :][:, None, :, None].broadcast_to([P, NB, LANE, E4]),
                              ALU.mult).then_inc(spread_ok, 1)
            dve.tensor_tensor(f1_spread, fj[:, 0, :][:, None, :].broadcast_to([P, QUAD, T]),
                              quads[:, ::LANE][:, :, None].broadcast_to([P, QUAD, T]), ALU.mult).then_inc(spread_ok, 1)
            dve.wait_ge(f2_ok, 2)
            dve.tensor_reduce(ext[:, 0:1], f2_all[:, :], AX.X, ALU.max)
            chain(dve.tensor_reduce(ext[:, 1:2], f2_all[:, :], AX.X, ALU.min))
            dve.tensor_tensor(ext[:, 2:10].rearrange("p (k q) -> p k q", k=2),
                              ext[:, 0:2][:, :, None].broadcast_to([P, 2, QUAD]),
                              quads[:, ::LANE][:, None, :].broadcast_to([P, 2, QUAD]), ALU.mult).then_inc(ext_ok, 1)
            dve.wait_ge(f2_ps_ok, 3)
            dve.tensor_copy(f1_rep[:, :, :], ps_s[:, 0:P].rearrange("p (g t) -> p g t", g=QUAD)).then_inc(f1_ok, 1)
            dve.wait_ge(ext_ps_ok, 1)
            dve.tensor_reduce(ext[:, 10:11], ps_f[:, P:P + 4], AX.X, ALU.max)
            chain(dve.tensor_reduce(ext[:, 11:12], ps_f[:, P + 4:P + 8], AX.X, ALU.min))
            chain(dve.tensor_scalar(ext[:, 12:14], ext[:, 10:12], 1.0 / LANE, None, ALU.mult))
            top = ext[:, 12:13]
            dve.tensor_scalar(wrong[:, 0:1], top, ext[:, 13:14], F2_RANGE, ALU.subtract, ALU.is_gt)
            chain(dve.tensor_scalar(tmp[:, 2], fj[:, 1], top, None, ALU.subtract))
            dve.tensor_scalar(tmp[:, 3], tmp[:, 2], SLOPE, None, ALU.mult).then_inc(arg_ok, 1)
            chain(dve.tensor_scalar(tmp[:, 6], fj[:, 0], top, None, ALU.add))
            dve.scalar_tensor_tensor(out=tmp[:, 7], in0=tmp[:, 6], scalar=SLOPE, in1=tmp[:, 6],
                                     op0=ALU.mult, op1=ALU.max).then_inc(arg_ok, 1)
            dve.wait_ge(arg_ok, 2)
            dve.tensor_tensor(tmp[:, 4], tmp[:, 6], tmp[:, 7], ALU.subtract).then_inc(arg_ok, 1)
            dve.scalar_tensor_tensor(out=tmp[:, 5], in0=tmp[:, 6], scalar=SLOPE, in1=tmp[:, 7],
                                     op0=ALU.mult, op1=ALU.subtract).then_inc(arg_ok, 1)
            dve.wait_ge(temp_ok, 1)
            chain(dve.tensor_scalar(coe[:, :], coe[:, :], 1.0, None, ALU.add))
            chain(dve.reciprocal(coe[:, :], coe[:, :]))
            one_less, minus_c3, one_less_c1, c0_rest, h0_share = (cmix[:, n:n + 1] for n in range(5))
            dve.tensor_scalar(one_less, coe[:, 2:3], -1.0, 1.0, ALU.mult, ALU.add)
            dve.tensor_scalar(minus_c3, coe[:, 3:4], -1.0, None, ALU.mult)
            dve.tensor_scalar(h0_share, coe[:, 0:1], -1.0, 1.0, ALU.mult, ALU.add)
            chain(dve.tensor_scalar(one_less_c1, coe[:, 1:2], -1.0, 1.0, ALU.mult, ALU.add))
            dve.tensor_tensor(c0_rest, one_less_c1, coe[:, 0:1], ALU.mult)
            dve.tensor_tensor(h0_share, one_less_c1, h0_share, ALU.mult)
            dve.wait_ge(exp_ok, 2)
            chain(dve.tensor_scalar(bdh[:, :, :], bd[:, :, :], S_H, None, ALU.mult))

            def scale_rows(b):
                if b >= 2:
                    dve.wait_ge(low_ok, b - 1)
                for k in range(2):
                    dve.tensor_tensor(scaled[:, 2 * (b % 2) + k].rearrange("p (e f) -> p e f", e=E4),
                                      h_all[:, E4 * b:E4 * (b + 1), :],
                                      bdh[:, k, E4 * b:E4 * (b + 1)][:, :, None].broadcast_to([P, E4, F]),
                                      ALU.mult).then_inc(scaled_ok, 1)

            def low_rows(b):
                dve.wait_ge(high_ok, 2 * b + 2)
                for k, dst in enumerate((xb, xd)):
                    ins = dve.tensor_tensor(dst[:, E4 * b:E4 * (b + 1), LO:LO + F],
                                            scaled[:, 2 * (b % 2) + k].rearrange("p (e f) -> p e f", e=E4),
                                            dst[:, E4 * b:E4 * (b + 1), 0:F], ALU.subtract)
                ins.then_inc(low_ok, 1)

            scale_rows(0)
            for b in range(NB):
                if b + 1 < NB:
                    scale_rows(b + 1)
                low_rows(b)
            chain(dve.tensor_tensor(tmp[:, 0:2], bd[:, :, :], bd[:, :, :], ALU.mult))
            chain(dve.tensor_scalar(tmp[:, 2:4], tmp[:, 0:2], S_SQ, None, ALU.mult))
            for k, dst in enumerate((xb, xd)):
                dve.tensor_copy(dst[:, :, F:F + 1], bdh[:, k, :][:, :, None])
                chain(dve.tensor_copy(dst[:, :, F + 1:F + 2], tmp[:, 2 + k][:, :, None]))
                dve.tensor_tensor(dst[:, :, LO + F:LO + F + 1], bdh[:, k, :][:, :, None], dst[:, :, F:F + 1], ALU.subtract)
                dve.tensor_tensor(dst[:, :, LO + F + 1:LO + F + 2], tmp[:, 2 + k][:, :, None], dst[:, :, F + 1:F + 2],
                                  ALU.subtract)
                dve.memset(dst[:, :, CNT:CNT + 2], 1.0)
            chain(dve.tensor_tensor(tmp[:, 0:2], ac[:, :, :], ac[:, :, :], ALU.mult))
            for k, vals in enumerate((POS_VAL, NEG_VAL)):
                for q in range(2):
                    dve.tensor_scalar(ac1[:, k, q::2], ac[:, k, q::2], 1.0 / (S_H * vals[q]), None, ALU.mult)
                    dve.tensor_scalar(acsq[:, k, q::2], tmp[:, k, q::2], 1.0 / (S_SQ * vals[q]), None, ALU.mult)
                    dve.tensor_scalar(ac2[:, k, q::2], ac[:, k, q::2], 1.0 / (S_F * vals[q]), None, ALU.mult)
            dve.tensor_scalar(bdf[:, :, :], bd[:, :, :], S_F, None, ALU.mult).then_inc(ready_ok, 1)

            def edges(p, q, half):
                n = 2 * q + half
                dve.wait_ge(adj_in[n], 64 * (p + 1))
                dve.tensor_scalar(edge[:, q, 2 * JQ * half:2 * JQ * (half + 1)], adj_ring[:, n, :], 1.0,
                                  float(POS[q] | NEG[q]), ALU.is_ge, ALU.mult).then_inc(edge_ok, 1)

            def encode(p):
                for q in range(2):
                    dve.wait_ge(side_ok, 2 * p + q + 1)
                    dve.wait_ge(edge_ok, 4 * p + 2 * q + 2)
                    dve.scalar_tensor_tensor(out=edge[:, q, :].bitcast(I32), in0=side[:, q, :].bitcast(I32),
                                             scalar=word(POS[q]), in1=edge[:, q, :].bitcast(I32),
                                             op0=ALU.bitwise_xor, op1=ALU.bitwise_and).then_inc(side_used, 1)
                dve.wait_ge(side_used, 2 * p + 4)
                dve.tensor_tensor(edge[:, 0, :].bitcast(I32), edge[:, 0, :].bitcast(I32), edge[:, 1, :].bitcast(I32),
                                  ALU.bitwise_or).then_inc(merged, 1)
                dve.wait_ge(merged, p + 1)
                dve.transpose(both_t[:, :, :].rearrange("p b (g c) -> p g b c", g=QUAD),
                              edge[:, 0, :].bitcast(I32).rearrange("p (g b r) -> p g b r", g=QUAD, b=NB))\
                    .then_inc(both_ok, 1)

            def flags_of(src, n, q):
                for half in range(2):
                    for k, bit in enumerate((POS[q], NEG[q])):
                        s = 4 * q + 2 * half + k
                        dve.wait_ge(flags_used, 8 * n + s + 1)
                        dve.tensor_scalar(flags[:, s % RING], src[:, 4 * half:4 * half + 4, :], word(bit), None,
                                          ALU.bitwise_and).then_inc(flags_ok, 1)

            def steps(sem_, base):
                at = [0]

                def step(ins):
                    at[0] += 1
                    ins.then_inc(sem_, 1)

                def settle():
                    dve.wait_ge(sem_, base + at[0])
                return step, settle, at

            def pair_feat(i, h):
                p = 2 * i + h
                pair = bass.ds(4 * i + 2 * h, 2)
                one = [bass.ds(4 * i + 2 * h + q, 1) for q in range(2)]
                step, settle, at = steps(step1, STEPS1 * p)
                for q in range(2):
                    dve.wait_ge(sums_used, 2 * p + q + 3)
                    step(dve.tensor_scalar(acc[:, q, :], ev[:, q, 0, 0:2 * LO], ac1[:, 0, one[q]], None, ALU.mult))
                step(dve.tensor_tensor(small[:, 0, :].rearrange("p (q k) -> p q k", q=2), ev[:, :, :, F + 1],
                                       ev[:, :, :, LO + F + 1], ALU.add))
                step(dve.tensor_copy(cnt[:, pair, :], ev[:, :, :, CNT]))
                settle()
                for q in range(2):
                    step(dve.scalar_tensor_tensor(out=acc[:, q, :], in0=ev[:, q, 1, 0:2 * LO], scalar=ac1[:, 1, one[q]],
                                                  in1=acc[:, q, :], op0=ALU.mult, op1=ALU.add))
                step(dve.tensor_tensor(small[:, 1, :].rearrange("p (q k) -> p q k", q=2),
                                       small[:, 0, :].rearrange("p (q k) -> p q k", q=2),
                                       acsq[:, :, pair].rearrange("p k q -> p q k"), ALU.mult))
                settle()
                dve.tensor_tensor(num[:, :, :], acc[:, :, 0:F + 1], acc[:, :, LO:LO + F + 1], ALU.add).then_inc(ev_used, 1)
                step(dve.tensor_tensor(small[:, 2, 0:2], small[:, 1, 0:4:2], small[:, 1, 1:4:2], ALU.add))
                dve.wait_ge(ev_used, p + 2)
                step(dve.tensor_scalar(small[:, 3, 2:4], num[:, :, F], 1e-30, None, ALU.max))
                settle()
                step(dve.reciprocal(rden[:, pair], small[:, 3, 2:4]))
                settle()
                step(dve.tensor_tensor(small[:, 3, 0:2], small[:, 2, 0:2], rden[:, pair], ALU.mult))
                settle()
                step(dve.scalar_tensor_tensor(out=rs[:, pair], in0=small[:, 3, 0:2], scalar=0.5, in1=rden[:, pair],
                                              op0=ALU.mult, op1=ALU.mult))
                settle()
                step(dve.tensor_scalar(small[:, 4, 0:2], rs[:, pair], -1.0, one_less, ALU.mult, ALU.add))
                settle()
                dve.wait_ge(h_ok, p + 1)
                for q in range(2):
                    ins = dve.tensor_scalar(rows[:, h, q, :], rows[:, h, q, :], small[:, 4, q:q + 1], None, ALU.mult)
                step(ins)
                settle()
                dve.wait_ge(feat_free, p + 1)
                for q in range(2):
                    ins = dve.scalar_tensor_tensor(out=feat[:, h, q, :], in0=num[:, q, 0:F], scalar=rden[:, one[q]],
                                                   in1=rows[:, h, q, :], op0=ALU.mult, op1=ALU.add)
                ins.then_inc(row_used, 1)
                dve.wait_ge(row_used, p + 1)
                step(dve.tensor_scalar(acc[:, :, 0:F], feat[:, h], THRESH, -THRESH, ALU.min, ALU.max))
                settle()
                dve.tensor_tensor(feat[:, h], feat[:, h], acc[:, :, 0:F], ALU.subtract).then_inc(feat_ok, 1)
                assert at[0] == STEPS1, at

            def low(i, h):
                dve.wait_ge(feat_ok, 2 * i + h + 1)
                dve.wait_ge(hi_ok, 2 * i + h + 1)
                for q in range(2):
                    t = bass.ds(4 * i + 2 * h + q, 1)
                    for k, dst in enumerate((fb, fd)):
                        ins = dve.scalar_tensor_tensor(out=dst[:, t, F:2 * F], in0=feat[:, h, q:q + 1, :], scalar=bdf[:, k, t],
                                                       in1=dst[:, t, 0:F], op0=ALU.mult, op1=ALU.subtract)
                ins.then_inc(feats_ok, 1)

            def front(p, i=None, h=None):
                if i is not None:
                    dve.wait_ge(saved, p)
                for q in range(2):
                    for half in range(2):
                        edges(p, q, half)
                encode(p)
                dve.wait_ge(both_ok, p + 1)
                flags_of(both_t, p, 0)
                if i is not None:
                    pair_feat(i, h)
                flags_of(both_t, p, 1)
                if i is not None:
                    low(i, h)

            front(0)
            with dve.Fori(0, NB - 1) as i:
                front(2 * i + 1, i, 0)
                front(2 * i + 2, i, 1)
            front(PAIRS - 1, NB - 1, 0)

            dve.wait_ge(saved, PAIRS)
            flags_of(codes[:, 0], PAIRS, 0)
            pair_feat(NB - 1, 1)
            low(NB - 1, 1)
            flags_of(codes[:, 0], PAIRS, 1)
            dve.tensor_tensor(ac2[:, :, :], ac2[:, :, :], rden[:, None, :].broadcast_to([P, 2, T]), ALU.mult)
            chain(dve.tensor_scalar(wmix[:, :], rs[:, :], coe[:, 1:2], c0_rest, ALU.mult, ALU.add))
            dve.wait_ge(count_ok, 2 * T)
            for q in range(2):
                chain(dve.tensor_scalar(rows_n[:, q::2], cnt[:, q::2, 0], 1.0 / POS_VAL[q], None, ALU.mult))
                chain(dve.scalar_tensor_tensor(out=rows_n[:, q::2], in0=cnt[:, q::2, 1], scalar=1.0 / NEG_VAL[q],
                                               in1=rows_n[:, q::2], op0=ALU.mult, op1=ALU.add))
            dve.tensor_reduce(wrong[:, 1:2], nz[:, :], AX.X, ALU.add)
            chain(dve.tensor_reduce(wrong[:, 2:3], rows_n[:, :], AX.X, ALU.add))
            chain(dve.tensor_tensor(wrong[:, 1:2], wrong[:, 1:2], wrong[:, 2:3], ALU.subtract))
            chain(dve.tensor_scalar(rows_n[:, :], rows_n[:, :], 0.0, None, ALU.is_equal))
            chain(dve.tensor_reduce(wrong[:, 2:3], rows_n[:, :], AX.X, ALU.add))
            chain(dve.tensor_tensor(wrong[:, 1:2], wrong[:, 1:2], wrong[:, 2:3], ALU.add))
            dve.tensor_tensor(wrong[:, 3:4], wrong[:, 0:1], wrong[:, 1:2], ALU.add).then_inc(wrong_ok, 1)

            def pair_out(i, h):
                p = 2 * i + h
                one = [bass.ds(4 * i + 2 * h + q, 1) for q in range(2)]
                step, settle, at = steps(step2, STEPS2 * p)
                dve.wait_ge(aux_in[h], 144 * (i + 1))
                step(dve.scalar_tensor_tensor(out=x_rows[:, h], in0=h0_rows[:, h], scalar=h0_share, in1=x_rows[:, h],
                                              op0=ALU.mult, op1=ALU.add))
                for q in range(2):
                    dve.wait_ge(sums_used, 2 * (PAIRS + p) + q + 3)
                    step(dve.tensor_scalar(acc[:, q, 0:W2], ev[:, q, 0, 0:W2], ac2[:, 0, one[q]], None, ALU.mult))
                settle()
                for q in range(2):
                    ins = dve.scalar_tensor_tensor(out=acc[:, q, 0:W2], in0=ev[:, q, 1, 0:W2], scalar=ac2[:, 1, one[q]],
                                                   in1=acc[:, q, 0:W2], op0=ALU.mult, op1=ALU.add)
                ins.then_inc(ev_used, 1)
                dve.wait_ge(ev_used, PAIRS + p + 2)
                step(dve.tensor_tensor(num[:, :, 0:F], acc[:, :, 0:F], acc[:, :, F:2 * F], ALU.add))
                settle()
                step(dve.scalar_tensor_tensor(out=feat_rows[:, h], in0=num[:, :, 0:F], scalar=minus_c3, in1=feat_rows[:, h],
                                              op0=ALU.mult, op1=ALU.add))
                step(dve.scalar_tensor_tensor(out=x_rows[:, h], in0=num[:, :, 0:F], scalar=coe[:, 1:2], in1=x_rows[:, h],
                                              op0=ALU.mult, op1=ALU.add))
                settle()
                dve.wait_ge(out_done[h], 64 * i + 64)
                for q in range(2):
                    ins = dve.scalar_tensor_tensor(out=y_rows[:, h, q], in0=feat_rows[:, h, q], scalar=wmix[:, one[q]],
                                                   in1=x_rows[:, h, q], op0=ALU.mult, op1=ALU.add)
                ins.then_inc(y_ok, 1)
                assert at[0] == STEPS2, at

            def front2(p, i, h):
                src = codes[:, bass.ds(p, 1)].rearrange("p o b i -> p (o b) i")
                flags_of(src, PAIRS + p, 0)
                pair_out(i, h)
                flags_of(src, PAIRS + p, 1)

            with dve.Fori(0, NB - 1) as i:
                front2(2 * i + 1, i, 0)
                front2(2 * i + 2, i, 1)
            front2(PAIRS - 1, NB - 1, 0)
            pair_out(NB - 1, 1)
            dve.wait_ge(wrong_ps_ok, 1)
            chain(dve.tensor_scalar(wrong[0:1, 0:1], ps_s[0:1, 0:1], 0.5, None, ALU.is_gt))
            dve.tensor_copy(flag_i[:, :], wrong[0:1, 0:1]).then_inc(flag_ok, 1)

            def root_refined(var, root, scratch, inv):
                chain_g(dve.reciprocal(scratch, root))
                chain_g(dve.tensor_tensor(scratch, var, scratch, ALU.mult))
                chain_g(dve.tensor_tensor(scratch, root, scratch, ALU.add))
                chain_g(dve.tensor_scalar(scratch, scratch, 0.5, None, ALU.mult))
                chain_g(dve.reciprocal(inv, scratch))

            def chain_g(ins):
                dve.drain()

            def g_product(n):
                for k in range(8):
                    after(dve, g_wt_ps, 8 * n + k + 1)
                    dve.tensor_copy(g_wt, ps_t[:, 0]).then_inc(g_wt_ok, 1)
                after(dve, g_prod, 8 * n + 8)

            def g_softmax(n, t):
                after(dve, g_adj_in, 16 * (n + 1))
                chain_g(dve.tensor_scalar(g_w, g_f2, g_f1[:, bass.ds(t, 1)], None, ALU.add))
                chain_g(dve.scalar_tensor_tensor(out=g_w, in0=g_w, scalar=SLOPE, in1=g_w, op0=ALU.mult, op1=ALU.max))
                chain_g(dve.tensor_scalar(g_t, g_adj, 0.0, -NEG_INF, ALU.is_gt, ALU.mult))
                chain_g(dve.scalar_tensor_tensor(out=g_w, in0=g_t, scalar=NEG_INF, in1=g_w, op0=ALU.add, op1=ALU.add))
                chain_g(dve.tensor_reduce(g_s[:, 0:1], g_w, AX.X, ALU.max))
                dve.tensor_scalar(g_s[:, 1:2], g_s[:, 0:1], -1.0, None, ALU.mult).then_inc(g_scored, 1)
                after(dve, g_exp, n + 1)
                chain_g(dve.reciprocal(g_s[:, 3:4], g_s[:, 2:3]))
                dve.tensor_scalar(g_w, g_w, g_s[:, 3:4], None, ALU.mult).then_inc(g_w_ok, 1)

            with general(dve):
                dve.wait_ge(g_in, 80)
                dve.memset(g_s[:, 5:6], -1.0)
                for t in range(T):
                    ins = dve.bn_stats(g_st[:, t, :], g_x[:, t, :])
                chain_g(ins)
                for t in range(T):
                    ins = dve.bn_aggr(g_mv[:, t, :], g_st[:, t, :])
                chain_g(ins)
                dve.tensor_scalar(g_tmp[:, 0], g_mv[:, :, 1], EPS, None, ALU.add).then_inc(g_var, 1)
                dve.wait_ge(g_root, 1)
                root_refined(g_tmp[:, 0], g_tmp[:, 1], g_tmp[:, 2], g_tmp[:, 3])
                for t in range(T):
                    ins = dve.tensor_scalar(g_h[:, t, :], g_x[:, t, :], g_mv[:, t, 0:1], g_tmp[:, 3, t:t + 1],
                                            ALU.subtract, ALU.mult)
                chain_g(ins)
                dve.tensor_scalar(g_h, g_h, 0.0, None, ALU.max)
                dve.tensor_copy(g_a2, g_a12[:, 1:2].broadcast_to([P, P])).then_inc(g_hn, 1)
                for b in range(NB):
                    dve.wait_ge(g_turned, b + 1)
                    dve.tensor_copy(g_ht, ps_t[:, 0]).then_inc(g_t_ok, 1)
                    dve.wait_ge(g_f, b + 1)
                    chain_g(dve.tensor_copy(g_f2[:, 512 * b:512 * (b + 1)], ps_t[:, 1]))
                chain_g(dve.tensor_copy(g_f1, ps_f[:, 0:T]))

                with dve.Fori(0, T) as t:
                    one = bass.ds(t, 1)
                    g_softmax(t, t)
                    g_product(t)
                    after(dve, g_sq, t + 1)
                    chain_g(dve.tensor_scalar(g_rs[:, one], g_s[:, 4:5], 0.5, None, ALU.mult))
                    chain_g(dve.tensor_scalar(g_s[:, 8:9], g_rs[:, one], -1.0, one_less, ALU.mult, ALU.add))
                    chain_g(dve.scalar_tensor_tensor(out=g_feat[:, one, :], in0=g_h[:, one, :], scalar=g_s[:, 8:9],
                                                     in1=ps_s[:, None, 0:F], op0=ALU.mult, op1=ALU.add))
                    chain_g(dve.tensor_scalar(g_wt[:, 0:F], g_feat[:, one, :].rearrange("p o f -> p (o f)"), THRESH, -THRESH,
                                              ALU.min, ALU.max))
                    chain_g(dve.tensor_tensor(g_feat[:, one, :], g_feat[:, one, :], g_wt[:, None, 0:F], ALU.subtract))

                with dve.Fori(0, T) as t:
                    one = bass.ds(t, 1)
                    g_softmax(T + t, t)
                    g_product(T + t)
                    after(dve, g_sq, T + t + 1)
                    pu, odd = ps_s[:, None, 0:F], g_wt[:, None, 0:F]
                    chain_g(dve.scalar_tensor_tensor(out=g_x[:, one, :], in0=g_h0[:, one, :], scalar=h0_share,
                                                     in1=g_x[:, one, :], op0=ALU.mult, op1=ALU.add))
                    chain_g(dve.scalar_tensor_tensor(out=odd, in0=pu, scalar=minus_c3, in1=g_feat[:, one, :],
                                                     op0=ALU.mult, op1=ALU.add))
                    chain_g(dve.scalar_tensor_tensor(out=g_x[:, one, :], in0=pu, scalar=coe[:, 1:2], in1=g_x[:, one, :],
                                                     op0=ALU.mult, op1=ALU.add))
                    chain_g(dve.tensor_scalar(g_s[:, 8:9], g_rs[:, one], coe[:, 1:2], c0_rest, ALU.mult, ALU.add))
                    chain_g(dve.scalar_tensor_tensor(out=g_x[:, one, :], in0=odd, scalar=g_s[:, 8:9], in1=g_x[:, one, :],
                                                     op0=ALU.mult, op1=ALU.add))
                    chain_g(dve.tensor_copy(g_ht[:, 0:F], g_x[:, one, :].rearrange("p o f -> p (o f)")))
                    chain_g(dve.bn_stats(g_st[:, 0, :], g_ht[:, 0:F]))
                    chain_g(dve.bn_aggr(g_mv[:, 0, :], g_st[:, 0, :]))
                    dve.tensor_scalar(g_s[:, 6:7], g_mv[:, 0, 1:2], EPS, None, ALU.add).then_inc(g_var, 1)
                    after(dve, g_root, t + 2)
                    root_refined(g_s[:, 6:7], g_s[:, 7:8], g_s[:, 8:9], g_s[:, 9:10])
                    chain_g(dve.tensor_scalar(g_ht[:, 0:F], g_ht[:, 0:F], g_mv[:, 0, 0:1], g_s[:, 9:10],
                                              ALU.subtract, ALU.mult))
                    dve.tensor_scalar(g_ht[:, 0:F], g_ht[:, 0:F], 0.0, None, ALU.max).then_inc(g_hn, 1)
                    after(dve, g_turned, NB + t + 1)
                    dve.tensor_copy(g_ht[:, P:2 * P], ps_f[:, 0:P]).then_inc(g_t_ok, 1)
                    after(dve, g_f, NB + t + 1)
                    chain_g(dve.tensor_tensor(g_msg[:, one, :], ps_t[:, 1, 0:F][:, None, :], g_bm[:, None, :], ALU.add))

                with dve.Fori(0, T) as t:
                    one = bass.ds(t, 1)
                    n = 2 * T + t
                    after(dve, g_adj_in, 16 * (n + 1))
                    chain_g(dve.tensor_tensor(g_t, g_adj, g_adj, ALU.mult))
                    chain_g(dve.tensor_scalar(g_t, g_t, 1e-4, 0.02, ALU.is_lt, ALU.mult))
                    chain_g(dve.tensor_tensor(g_w, g_t, g_adj, ALU.add))
                    dve.reciprocal(g_w, g_w).then_inc(g_scored, 1)
                    after(dve, g_exp, n + 1)
                    dve.scalar_tensor_tensor(out=g_w, in0=g_adj, scalar=1.0, in1=g_w, op0=ALU.is_lt,
                                             op1=ALU.mult).then_inc(g_w_ok, 1)
                    g_product(n)
                    chain_g(dve.tensor_tensor(g_x[:, one, :], ps_s[:, None, 0:F], g_x[:, one, :], ALU.add))
                dve.sem_inc(g_done, 1)


_INS = ['x', 'adj', 'L0_gnn_h0', 'L0_gnn_a', 'L0_gnn_temp', 'L1_gnn_W', 'L1_gnn_B']


def kernel(**inputs):
    import numpy as _np
    import concourse.bacc as _bacc
    from concourse import mybir as _mybir
    from concourse.bass_utils import run_bass_kernel_spmd as _run

    nc = _bacc.Bacc("TRN2", target_bir_lowering=False, num_devices=1)
    arrays, args = {}, []
    for name in _INS:
        a = _np.ascontiguousarray(inputs[name])
        arrays[f"in_{name}_dram"] = a
        args.append(nc.dram_tensor(f"in_{name}_dram", a.shape, _mybir.dt.from_np(a.dtype), kind="ExternalInput").ap())
    out = nc.dram_tensor("out_dram", (4096, 128), _mybir.dt.float32, kind="ExternalOutput").ap()
    build(nc, *args, out)
    r = _run(nc, [arrays], core_ids=[0])
    return r.results[0]["out_dram"]
```

```python
import concourse.bass as bass
from concourse import mybir
from contextlib import ExitStack
import numpy as np

FP32, FP16, FP8 = mybir.dt.float32, mybir.dt.float16, mybir.dt.float8e4
U8, I8, I32, U32 = mybir.dt.uint8, mybir.dt.int8, mybir.dt.int32, mybir.dt.uint32
ALU, ACT, AX = mybir.AluOpType, mybir.ActivationFunctionType, mybir.AxisListType

P = 128
N, F = 4096, 128
T = N // P
PAIRS = T // 2
QUAD = 4
LANE = P // QUAD
JQ = N // QUAD
NB = JQ // P
E4 = 4
SLOPE, EPS, THRESH, NEG_INF = 0.2, 1e-5, 1e-6, -9e15
F2_RANGE = 10.0

S_H = 4096.0
S_SQ = 32768.0
S_F = 2048.0
W1 = 262
LO = 130
CNT = 260
W2 = 256

POS = (0x40, 0x10)
NEG = (0x20, 0x08)
POS_VAL = (2.0, 2.0 ** -5)
NEG_VAL = (2.0 ** -3, 2.0 ** -6)


RING = 4
POOL_GROUPS = ((3,), (3,))
STEPS1 = 15
STEPS2 = 6


def word(byte):
    return int(byte) * 0x01010101


def build(nc, x, adj, h0, a, temp, w_msg, b_msg, out):
    feat_scratch = nc.dram_tensor("feat_scratch", (PAIRS, P, 2 * F), FP32).ap()
    ctx = ExitStack()
    with ctx:
        def sb(name, shape, dt):
            return ctx.enter_context(nc.sbuf_tensor(name, shape, dt))

        def sem(name):
            return ctx.enter_context(nc.semaphore(name))

        codes = sb("codes", [P, PAIRS, NB, P], I32)
        xb = sb("xb", [P, T, W1], FP16)
        xd = sb("xd", [P, T, W1], FP16)
        fb = sb("fb", [P, T, W2], FP16)
        fd = sb("fd", [P, T, W2], FP16)
        adj_ring = sb("adj_ring", [P, 4, 2 * JQ], FP32)
        edge = sb("edge", [P, 2, N], U8)
        side = sb("side", [P, 2, N], I8)
        both_t = sb("both_t", [P, NB, P], I32)
        flags = sb("flags", [P, RING, 4, P], I32)
        f2_all = sb("f2_all", [P, JQ], FP32)
        f1_rep = sb("f1_rep", [P, QUAD, T], FP32)
        nz = sb("nz", [P, 2 * T], FP32)
        cnt = sb("cnt", [P, T, 2], FP32)
        ac = sb("ac", [P, 2, T], FP32)
        ac1 = sb("ac1", [P, 2, T], FP32)
        ac2 = sb("ac2", [P, 2, T], FP32)
        minus_f1 = ac2
        rden = sb("rden", [P, T], FP32)
        rs = sb("rs", [P, T], FP32)
        wmix = sb("wmix", [P, T], FP32)
        bd = sb("bd", [P, 2, T], FP32)
        bdh = sb("bdh", [P, 2, T], FP32)
        threshold = sb("threshold", [P, 2], FP32)
        bdf = sb("bdf", [P, 2, T], FP32)
        rstd = sb("rstd", [P, T], FP32)
        nmr = sb("nmr", [P, T], FP32)
        coe = sb("coe", [P, 5], FP32)
        cmix = sb("cmix", [P, 6], FP32)
        small = sb("small", [P, 5, 4], FP32)
        acsq = sb("acsq", [P, 2, T], FP32)
        ones_col = sb("ones_col", [P, 1], FP32)
        wrong = sb("wrong", [P, 4], FP32)
        rows_n = sb("rows_n", [P, T], FP32)
        flag_i = sb("flag_i", [1, 1], I32)
        rows = sb("rows", [P, 2, 2, F], FP32)
        ev = sb("ev", [P, 2, 2, W1], FP32)
        acc = sb("acc", [P, 2, LO * 2], FP32)
        num = sb("num", [P, 2, F + 1], FP32)
        feat = sb("feat", [P, 2, 2, F], FP32)
        print("SBUF left", nc.sbuf_bytes_remaining if not callable(nc.sbuf_bytes_remaining) else nc.sbuf_bytes_remaining())

        early = codes[:, PAIRS // 2:, :, :].bitcast(FP32).rearrange("p s b i -> p (s b i)")
        x_all = early[:, 0:T * F].rearrange("p (t f) -> p t f", f=F)
        h_all = early[:, T * F:2 * T * F].rearrange("p (t f) -> p t f", f=F)
        scrap = fb[:, :, :].rearrange("p t w -> p (t w)").bitcast(FP32)
        h_t = scrap[:, 0:1024].rearrange("p (s w) -> p s w", s=2)
        spread = scrap[:, 1024:2048]
        scaled = scrap[:, 2048:4096].rearrange("p (s w) -> p s w", s=4)
        scrap2 = fd[:, :, :].rearrange("p t w -> p (t w)").bitcast(FP32)
        ident = scrap2[:, 0:128]
        quads = scrap2[:, 128:256]
        lanes = scrap2[:, 256:384].rearrange("p (a c) -> p a c", a=QUAD)
        ones = scrap2[:, 384:512]
        f1_spread = scrap2[:, 512:640].rearrange("p (g t) -> p g t", g=QUAD)
        stats = scrap2[:, 640:640 + 6 * T].rearrange("p (t s) -> p t s", s=6)
        mv = scrap2[:, 1024:1024 + 2 * T].rearrange("p (t s) -> p t s", s=2)
        a12 = scrap2[:, 1100:1102]
        fj = scrap2[:, 1104:1104 + 2 * T].rearrange("p (k t) -> p k t", k=2)
        tmp = scrap2[:, 1200:1200 + 8 * T].rearrange("p (n t) -> p n t", t=T)
        nmean = scrap2[:, 1460:1460 + T]
        ext = scrap2[:, 1500:1504]
        ext_rows = scrap2[:, 1600:1600 + 2 * P].rearrange("p (k c) -> p k c", k=2)
        bdx = scrap2[:, 1900:1900 + 2 * T].rearrange("p (k t) -> p k t", k=2)

        g_rows = codes[:, :, :, :].bitcast(FP32).rearrange("p s b i -> p (s b i)")
        g_f2, g_x, g_h0, g_msg = (g_rows[:, N * n:N * (n + 1)] for n in range(4))
        g_x, g_h0, g_msg = (w.rearrange("p (t f) -> p t f", f=F) for w in (g_x, g_h0, g_msg))
        g_h = scrap.rearrange("p (t f) -> p t f", f=F)
        g_feat = scrap2.rearrange("p (t f) -> p t f", f=F)
        g_adj = adj_ring[:, 0:2, :].rearrange("p s j -> p (s j)")
        g_w = xb[:, :, :].rearrange("p t w -> p (t w)").bitcast(FP32)[:, 0:N]
        g_t = xd[:, :, :].rearrange("p t w -> p (t w)").bitcast(FP32)[:, 0:N]
        g_more = adj_ring[:, 2:4, :].rearrange("p s j -> p (s j)")
        g_wt, g_ident, g_wm, g_bm, g_a2, g_ht = (g_more[:, 512 * n:512 * n + w] for n, w in
                                                 enumerate((512, P, F, F, P, 512)))
        g_st = g_more[:, 3072:3072 + 6 * T].rearrange("p (t s) -> p t s", s=6)
        g_mv = g_more[:, 3328:3328 + 2 * T].rearrange("p (t s) -> p t s", s=2)
        g_tmp = g_more[:, 3400:3400 + 5 * T].rearrange("p (n t) -> p n t", t=T)
        g_f1 = g_more[:, 3600:3600 + T]
        g_rs = g_more[:, 3640:3640 + T]
        g_a12 = g_more[:, 3680:3682]
        g_s = g_more[:, 3700:3712]

        ps = ctx.enter_context(nc.psum_tensor("ps", [P, 2, 2, 512], FP32))
        ps_more = ctx.enter_context(nc.psum_tensor("ps_more", [P, 4, 512], FP32))
        ps_t, ps_f, ps_s = ps_more[:, 0:2], ps_more[:, 2], ps_more[:, 3]

        x_in = [sem(f"x_in{c}") for c in range(NB // 2)]
        a_in = sem("a_in")
        adj_in = [sem(f"adj_in{s}") for s in range(4)]
        row_in = [sem(f"row_in{s}") for s in range(2)]
        aux_in = [sem(f"aux_in{s}") for s in range(2)]
        feat_out = [sem(f"feat_out{s}") for s in range(2)]
        out_done = [sem(f"out_done{s}") for s in range(2)]
        const_ok = sem("const_ok")
        v = sem("v")
        var_ok = sem("var_ok")
        root_ok = sem("root_ok")
        mean_ok = sem("mean_ok")
        h_chunk_ok = sem("h_chunk_ok")
        turned_ok = sem("turned_ok")
        h_t_ok = sem("h_t_ok")
        f_ok = sem("f_ok")
        spread_ok = sem("spread_ok")
        f2_ps_ok = sem("f2_ps_ok")
        f2_ok = sem("f2_ok")
        f1_ok = sem("f1_ok")
        ext_ok = sem("ext_ok")
        ext_ps_ok = sem("ext_ps_ok")
        arg_ok = sem("arg_ok")
        exp_ok = sem("exp_ok")
        temp_ok = sem("temp_ok")
        scaled_ok = sem("scaled_ok")
        high_ok = sem("high_ok")
        low_ok = sem("low_ok")
        ready_ok = sem("ready_ok")
        edge_ok = sem("edge_ok")
        count_ok = sem("count_ok")
        side_ok = sem("side_ok")
        pool_side_ok = sem("pool_side_ok")
        threshold_ok = sem("threshold_ok")
        side_used = sem("side_used")
        merged = sem("merged")
        both_ok = sem("both_ok")
        saved = sem("saved")
        flags_ok = sem("flags_ok")
        turn = sem("turn")
        flags_used = sem("flags_used")
        sums_used = sem("sums_used")
        ev_used = sem("ev_used")
        h_ok = sem("h_ok")
        row_used = sem("row_used")
        step1 = sem("step1")
        feat_ok = sem("feat_ok")
        hi_ok = sem("hi_ok")
        feats_ok = sem("feats_ok")
        step2 = sem("step2")
        y_ok = sem("y_ok")
        wrong_ok = sem("wrong_ok")
        wrong_ps_ok = sem("wrong_ps_ok")
        flag_ok = sem("flag_ok")
        g_in = sem("g_in")
        g_adj_in = sem("g_adj_in")
        g_const = sem("g_const")
        going_on = sem("going_on")
        g_seen = sem("g_seen")
        g_root = sem("g_root")
        g_var = sem("g_var")
        g_hn = sem("g_hn")
        g_turned = sem("g_turned")
        g_t_ok = sem("g_t_ok")
        g_f = sem("g_f")
        g_scored = sem("g_scored")
        g_exp = sem("g_exp")
        g_w_ok = sem("g_w_ok")
        g_sq = sem("g_sq")
        g_wt_ps = sem("g_wt_ps")
        g_wt_ok = sem("g_wt_ok")
        g_prod = sem("g_prod")
        g_done = sem("g_done")
        g_out = sem("g_out")
        block = ctx.enter_context(nc.Block())

        def after(eng, sem_, value):
            eng.wait_ge(sem_, value)
            eng.sem_inc(g_seen, 1)

        def general(eng):
            eng.wait_ge(flag_ok, 1)
            return eng.If(eng.value_load(flag_i[0:1, 0:1], min_val=0, max_val=1) == 1)

        adj_v = adj.rearrange("(g b c e) (a j) -> a b e c g j", g=QUAD, b=NB, c=LANE, e=E4, a=QUAD)
        x_v = x.rearrange("(g b c e) f -> g b c (e f)", g=QUAD, b=NB, c=LANE, e=E4)
        h0_v = h0.rearrange("(g b c e) f -> g b c (e f)", g=QUAD, b=NB, c=LANE, e=E4)
        out_v = out.rearrange("(g b c e) f -> g b c (e f)", g=QUAD, b=NB, c=LANE, e=E4)

        aux = adj_ring[:, :, :].rearrange("p s j -> p (s j)")
        h0_rows, x_rows, feat_rows, y_rows = (
            aux[:, 512 * n:512 * (n + 1)].rearrange("p (s e f) -> p s e f", s=2, e=2) for n in range(4))

        def pair_rows(view, b, h, g):
            return view[g, b, :, 2 * F * h:2 * F * (h + 1)]

        def lanes_of(tile, g):
            return tile[LANE * g:LANE * (g + 1)].rearrange("c e f -> c (e f)")

        @block.sync
        def _(sp):
            def load_adj(b, e, half, slot):
                for q in range(QUAD):
                    sp.dma_start(adj_ring[LANE * q:LANE * (q + 1), slot, :].rearrange("c (g j) -> c g j", g=2),
                                 adj_v[q, b, e, :, 2 * half:2 * half + 2, :]).then_inc(adj_in[slot], 16)

            def slot_free(t, half):
                sp.wait_ge(edge_ok, 2 * t + half + 1)
                sp.sem_inc(going_on, 1)
                sp.wait_ge(count_ok, 2 * t + half + 2)
                sp.sem_inc(going_on, 1)

            for b in range(0, NB, 2):
                for g in range(QUAD):
                    sp.dma_start(x_all[LANE * g:LANE * (g + 1), E4 * b:E4 * (b + 2), :]
                                 .rearrange("c (b e) f -> c b (e f)", b=2),
                                 x_v[g, b:b + 2].rearrange("b c w -> c b w")).then_inc(x_in[b // 2], 16)

            def load_rows(b, h):
                for g in range(QUAD):
                    sp.dma_start(lanes_of(rows[:, h], g), pair_rows(x_v, b, h, g)).then_inc(row_in[h], 16)

            def store_feat(b, h):
                sp.wait_ge(feat_ok, 2 * b + h + 1)
                sp.sem_inc(going_on, 1)
                sp.dma_start(feat_scratch[bass.ds(2 * b + h, 1)].rearrange("o p w -> (o p) w"),
                             feat[:, h].rearrange("p e f -> p (e f)")).then_inc(feat_out[h], 16)

            def load_tile(b, h, q, first=False):
                for half in range(2):
                    if not first:
                        slot_free(2 * (2 * b + h) - 2 + q, half)
                    load_adj(b, 2 * h + q, half, 2 * q + half)

            def turn_rows(b, h):
                store_feat(b, h)
                sp.wait_ge(row_used, 2 * b + h + 1)
                sp.sem_inc(going_on, 1)
                load_rows(b + 1, h)

            for q in range(2):
                load_tile(0, 0, q, first=True)
            for h in range(2):
                load_rows(0, h)
            for b, h in ((0, 1), (1, 0)):
                for q in range(2):
                    load_tile(b, h, q)
            with sp.Fori(0, NB - 2) as b:
                for h in range(2):
                    for q in range(2):
                        load_tile(b + 1 + h, 1 - h, q)
                    turn_rows(b, h)
            for q in range(2):
                load_tile(NB - 1, 1, q)
            for h in range(2):
                turn_rows(NB - 2, h)
            for h in range(2):
                store_feat(NB - 1, h)

            def load_aux(b, h):
                for g in range(QUAD):
                    sp.dma_start(lanes_of(h0_rows[:, h], g), pair_rows(h0_v, b, h, g)).then_inc(aux_in[h], 16)
                    sp.dma_start(lanes_of(x_rows[:, h], g), pair_rows(x_v, b, h, g)).then_inc(aux_in[h], 16)
                sp.dma_start(feat_rows[:, h].rearrange("p e f -> p (e f)"),
                             feat_scratch[bass.ds(2 * b + h, 1)].rearrange("o p w -> (o p) w")).then_inc(aux_in[h], 16)

            def store_out(b, h):
                sp.wait_ge(y_ok, 2 * b + h + 1)
                for g in range(QUAD):
                    sp.dma_start(pair_rows(out_v, b, h, g), lanes_of(y_rows[:, h], g)).then_inc(out_done[h], 16)

            slot_free(T - 1, 1)
            for s in range(2):
                sp.wait_ge(feat_out[s], 16 * (PAIRS // 2 + 1))
            load_aux(0, 0)
            load_aux(0, 1)
            with sp.Fori(0, NB - 1) as b:
                for h in range(2):
                    store_out(b, h)
                    load_aux(b + 1, h)
            for h in range(2):
                store_out(NB - 1, h)
            for s in range(2):
                sp.wait_ge(out_done[s], 64 * (NB + 1))

            with general(sp):
                rows_of = lambda m: m.rearrange("(t p) f -> p t f", p=P)
                sp.dma_start(g_x, rows_of(x)).then_inc(g_in, 16)
                sp.dma_start(g_h0, rows_of(h0)).then_inc(g_in, 16)
                sp.dma_start(g_wm, w_msg).then_inc(g_in, 16)
                sp.dma_start(g_bm, b_msg.rearrange("(o f) -> o f", o=1).broadcast_to([P, F])).then_inc(g_in, 16)
                sp.dma_start(g_a12, a.rearrange("(k f) o -> f (k o)", k=2), allow_slow_non_contiguous=True)\
                    .then_inc(g_in, 16)
                adj_rows = adj.rearrange("(t p) j -> t p j", p=P)
                for phase in range(3):
                    if phase:
                        sp.wait_ge(g_w_ok, T * phase)
                    sp.dma_start(g_adj, adj_rows[0]).then_inc(g_adj_in, 16)
                    with sp.Fori(0, T - 1) as t:
                        sp.wait_ge(g_w_ok, T * phase + t + 1)
                        sp.dma_start(g_adj, adj_rows[bass.ds(t + 1, 1)].rearrange("o p j -> (o p) j")).then_inc(g_adj_in, 16)
                sp.wait_ge(g_done, 1)
                sp.dma_start(rows_of(out), g_x).then_inc(g_out, 16)
                sp.wait_ge(g_out, 16)

        @block.gpsimd
        def _(pool):
            pool.memset(ident, 0.0).then_inc(const_ok, 1)
            pool.memset(quads, 0.0).then_inc(const_ok, 1)
            pool.memset(ones, 1.0).then_inc(const_ok, 1)
            pool.wait_ge(const_ok, 3)
            pool.affine_select(out=ident, in_=ident, compare_op=ALU.not_equal, fill=1.0, base=0,
                               pattern=[[-1, P]], channel_multiplier=1).then_inc(const_ok, 1)
            for q in range(QUAD):
                pool.wait_ge(const_ok, 4 + q)
                pool.memset(quads[LANE * q:LANE * (q + 1), LANE * q:LANE * (q + 1)], 1.0).then_inc(const_ok, 1)

            def save(p):
                pool.wait_ge(both_ok, p + 1)
                pool.tensor_copy(codes[:, bass.ds(p, 1), :, :], both_t[:, None, :, :]).then_inc(saved, 1)

            def compare(p):
                for q in range(2):
                    pool.wait_ge(side_used, 2 * p + q + 1)
                    pool.wait_ge(pool_side_ok, 2 * p + q + 1)
                    pool.tensor_copy(threshold[:, :], minus_f1[:, :, bass.ds(2 * p + q, 1)].rearrange("p g o -> p (g o)"))\
                        .then_inc(threshold_ok, 1)
                    pool.wait_ge(threshold_ok, 2 * p + q + 1)
                    pool.sem_inc(going_on, 1)
                    for g in POOL_GROUPS[q]:
                        last = pool.tensor_scalar(side[:, q, JQ * g:JQ * (g + 1)].bitcast(U8), f2_all[:, :],
                                                  threshold[:, g - 2:g - 1], 255.0, ALU.is_lt, ALU.mult)
                    last.then_inc(pool_side_ok, 1)

            pool.sem_inc(pool_side_ok, 1)
            pool.wait_ge(f2_ok, 2)
            pool.wait_ge(f1_ok, 2)
            compare(0)
            with pool.Fori(0, PAIRS - 1) as p:
                save(p)
                compare(p + 1)
            save(PAIRS - 1)

            with general(pool):
                pool.memset(g_ident, 0.0).then_inc(g_const, 1)
                pool.wait_ge(g_const, 1)
                pool.affine_select(out=g_ident, in_=g_ident, compare_op=ALU.not_equal, fill=1.0, base=0,
                                   pattern=[[-1, P]], channel_multiplier=1).then_inc(g_const, 1)

        @block.scalar
        def _(act):
            act.dma_start(a12, a.rearrange("(k f) o -> f (k o)", k=2), allow_slow_non_contiguous=True).then_inc(a_in, 16)
            act.dma_start(coe[:, :], temp.rearrange("(o k) -> o k", o=1).broadcast_to([P, 5])).then_inc(a_in, 16)
            for b in range(NB):
                act.wait_ge(mean_ok, b + 1)
                for t in range(E4 * b, E4 * (b + 1)):
                    last = act.activation(h_all[:, t, :], x_all[:, t, :], ACT.Relu, bias=nmean[:, t:t + 1])
                last.then_inc(h_chunk_ok, 1)
            act.wait_ge(var_ok, 1)
            act.activation(tmp[:, 1], tmp[:, 0], ACT.Sqrt).then_inc(root_ok, 1)

            def count(p, q, junk=ps_more[:, :, :]):
                for half in range(2):
                    n = 2 * q + half
                    act.wait_ge(adj_in[n], 64 * (p + 1))
                    act.wait_ge(count_ok, 4 * p + n + 1)
                    act.activation(junk.rearrange("p s j -> p (s j)"), adj_ring[:, n, :].bitcast(U32), ACT.Sign,
                                   accum_out=nz[:, bass.ds(4 * p + n, 1)]).then_inc(count_ok, 1)

            def compare(p, q):
                act.wait_ge(side_used, 2 * p + q + 1)
                for g in range(QUAD):
                    if g not in POOL_GROUPS[q]:
                        last = act.activation(side[:, q, JQ * g:JQ * (g + 1)], f2_all[:, :], ACT.Sign,
                                              bias=f1_rep[:, g, bass.ds(2 * p + q, 1)])
                last.then_inc(side_ok, 1)

            def drain(p, q, width):
                act.wait_ge(flags_used, 4 * (2 * p + q + 1) + RING)
                act.wait_ge(ev_used, p + 1)
                act.activation(ev[:, q, :, 0:width], ps[:, q, :, 0:width], ACT.Copy).then_inc(sums_used, 1)

            def h_again(i, h):
                act.wait_ge(row_in[h], 64 * (i + 1))
                for q in range(2):
                    t = bass.ds(4 * i + 2 * h + q, 1)
                    last = act.activation(rows[:, h, q, :], rows[:, h, q, :], ACT.Relu, scale=rstd[:, t], bias=nmr[:, t])
                last.then_inc(h_ok, 1)

            def high(i, h):
                act.wait_ge(feat_ok, 2 * i + h + 1)
                for q in range(2):
                    t = bass.ds(4 * i + 2 * h + q, 1)
                    for k, dst in enumerate((fb, fd)):
                        last = act.activation(dst[:, t, 0:F], feat[:, h, q:q + 1, :], ACT.Copy, scale=bdf[:, k, t])
                last.then_inc(hi_ok, 1)

            def turn(p, i, h, after_next=True):
                drain(p - 1, 1, W1)
                h_again(i, h)
                compare(p + 1, 1)
                count(p + 1, 1)
                drain(p, 0, W1)
                if after_next:
                    count(p + 2, 0)
                high(i, h)
                if after_next:
                    compare(p + 2, 0)

            act.sem_inc(count_ok, 1)
            for q in range(2):
                count(0, q, ps[:, :, :, :].rearrange("p q k j -> p (q k) j"))
            act.wait_ge(a_in, 32)
            act.activation(coe[:, :], coe[:, :], ACT.Exp, scale=-1.0).then_inc(temp_ok, 1)
            for n in range(2):
                act.wait_ge(f2_ps_ok, n + 1)
                act.activation(f2_all[:, 512 * n:512 * (n + 1)], ps_t[:, n], ACT.Copy).then_inc(f2_ok, 1)
            act.wait_ge(arg_ok, 4)
            act.activation(bd[:, :, :], tmp[:, 2:4], ACT.Exp).then_inc(exp_ok, 1)
            act.activation(ac[:, :, :], tmp[:, 4:6], ACT.Exp).then_inc(exp_ok, 1)
            act.wait_ge(f1_ok, 1)
            act.wait_ge(f2_ok, 2)
            for q in range(2):
                compare(0, q)
            for b in range(NB):
                for k, dst in enumerate((xb, xd)):
                    act.wait_ge(scaled_ok, 2 * b + k + 1)
                    act.activation(dst[:, E4 * b:E4 * (b + 1), 0:F],
                                   scaled[:, 2 * (b % 2) + k].rearrange("p (e f) -> p e f", e=E4),
                                   ACT.Copy).then_inc(high_ok, 1)
                if b in (NB // 2, NB - 2):
                    count(1, b // (NB - 2))
            for q in range(2):
                compare(1, q)
            drain(0, 0, W1)
            count(2, 0)
            compare(2, 0)
            with act.Fori(0, NB - 2) as i:
                turn(2 * i + 1, i, 0)
                turn(2 * i + 2, i, 1)
            turn(PAIRS - 3, NB - 2, 0)
            turn(PAIRS - 2, NB - 2, 1, after_next=False)
            drain(PAIRS - 2, 1, W1)
            h_again(NB - 1, 0)
            drain(PAIRS - 1, 0, W1)
            high(NB - 1, 0)
            drain(PAIRS - 1, 1, W1)
            h_again(NB - 1, 1)
            high(NB - 1, 1)
            with act.Fori(PAIRS, 2 * PAIRS) as p:
                for q in range(2):
                    drain(p, q, W2)

            with general(act):
                act.wait_ge(g_var, 1)
                act.activation(g_tmp[:, 1], g_tmp[:, 0], ACT.Sqrt).then_inc(g_root, 1)
                for phase in range(3):
                    with act.Fori(0, T) as t:
                        n = T * phase + t
                        after(act, g_scored, n + 1)
                        if phase < 2:
                            act.activation(g_w, g_w, ACT.Exp, bias=g_s[:, 1:2], accum_out=g_s[:, 2:3]).then_inc(g_exp, 1)
                            after(act, g_w_ok, n + 1)
                            act.activation(g_t, g_w, ACT.Square, accum_out=g_s[:, 4:5]).then_inc(g_sq, 1)
                        else:
                            act.activation(g_t, g_w, ACT.Square, bias=g_s[:, 5:6]).then_inc(g_sq, 1)
                            after(act, g_sq, n + 1)
                            act.activation(g_w, g_t, ACT.Exp, scale=-2.0).then_inc(g_exp, 1)
                        if phase == 1:
                            after(act, g_var, t + 2)
                            act.activation(g_s[:, 7:8], g_s[:, 6:7], ACT.Sqrt).then_inc(g_root, 1)

        @block.tensor
        def _(pe):
            pe.sem_inc(flags_used, RING)
            pe.wait_ge(const_ok, 8)
            pe.wait_ge(a_in, 32)

            def project(b):
                pe.wait_ge(h_t_ok, b + 1)
                for e in range(E4):
                    last = pe.matmul(ps_f[:, 2 * (E4 * b + e):2 * (E4 * b + e) + 2], h_t[:, b % 2, P * e:P * (e + 1)], a12,
                                     start=True, stop=True)
                last.then_inc(f_ok, 1)

            for b in range(NB):
                pe.wait_ge(h_chunk_ok, b + 1)
                if b >= 2:
                    pe.wait_ge(h_t_ok, b - 1)
                for e in range(E4):
                    last = pe.transpose(ps_t[:, b % 2, P * e:P * (e + 1)], h_all[:, E4 * b + e, :], ident)
                last.then_inc(turned_ok, 1)
                if b >= 1:
                    project(b - 1)
            project(NB - 1)
            pe.wait_ge(ext_ok, 1)
            pe.matmul(ps_f[:, P:3 * P], ones, ext_rows.rearrange("p k c -> p (k c)"), start=True, stop=True)\
                .then_inc(ext_ps_ok, 1)
            pe.wait_ge(spread_ok, 2)
            for n in range(2):
                pe.matmul(ps_t[:, n], quads, spread[:, 512 * n:512 * (n + 1)], start=True, stop=True).then_inc(f2_ps_ok, 1)
            pe.matmul(ps_s[:, 0:P], lanes.rearrange("p a c -> p (a c)"), f1_spread.rearrange("p g t -> p (g t)"),
                      start=True, stop=True).then_inc(f2_ps_ok, 1)

            def tile_sums(p, q, ops, width, gate):
                pe.wait_ge(sums_used, 2 * p + q + 1)
                for half in range(2):
                    for k in range(2):
                        s = 4 * q + 2 * half + k
                        pe.wait_ge(flags_ok, 8 * p + s + 1)
                        pe.sem_inc(turn, 1)
                        bytes_ = flags[:, s % RING].bitcast(FP8).rearrange("p b (i e) -> p b i e", e=E4)
                        for b in range(4):
                            for e in range(E4):
                                t = E4 * (4 * half + b) + e
                                if k == 0 and gate is not None:
                                    gate(t)
                                last = pe.matmul(ps[:, q, k, 0:width], bytes_[:, b, :, e], ops[k][:, t, 0:width],
                                                 start=(t == 0), stop=(t == T - 1))
                        last.then_inc(flags_used, 1)

            def rows_there(t):
                if t % E4 == 0:
                    pe.wait_ge(low_ok, t // E4 + 1)

            pe.wait_ge(count_ok, 5)
            pe.wait_ge(ready_ok, 1)
            tile_sums(0, 0, (xb, xd), W1, rows_there)
            tile_sums(0, 1, (xb, xd), W1, None)
            with pe.Fori(1, PAIRS) as p:
                for q in range(2):
                    tile_sums(p, q, (xb, xd), W1, None)

            def feats_there(t):
                if t % 8 == 0 or t == T - 2:
                    pe.wait_ge(feats_ok, min(t // 2 + 4, PAIRS - 1) if t < T - 2 else PAIRS)

            with pe.Fori(PAIRS, 2 * PAIRS) as p:
                for q in range(2):
                    tile_sums(p, q, (fb, fd), W2, feats_there if q == 0 else None)
            pe.wait_ge(wrong_ok, 1)
            pe.matmul(ps_s[0:1, 0:1], wrong[:, 3:4], ones_col[:, :], start=True, stop=True).then_inc(wrong_ps_ok, 1)

            with general(pe):
                pe.wait_ge(g_const, 2)
                for b in range(NB):
                    if b == 0:
                        pe.wait_ge(g_hn, 1)
                    for e in range(E4):
                        last = pe.transpose(ps_t[:, 0, P * e:P * (e + 1)], g_h[:, E4 * b + e, :], g_ident)
                    last.then_inc(g_turned, 1)
                    pe.wait_ge(g_t_ok, b + 1)
                    for e in range(E4):
                        pe.matmul(ps_f[:, E4 * b + e:E4 * b + e + 1], g_ht[:, P * e:P * (e + 1)], g_a12[:, 0:1],
                                  start=True, stop=True)
                    pe.matmul(ps_t[:, 1], g_a2, g_ht, start=True, stop=True).then_inc(g_f, 1)
                for phase, rhs in enumerate((g_h, g_feat, g_msg)):
                    with pe.Fori(0, T) as t:
                        n = T * phase + t
                        after(pe, g_w_ok, n + 1)
                        for k in range(8):
                            for c in range(4):
                                last = pe.transpose(ps_t[:, 0, P * c:P * (c + 1)], g_w[:, P * (4 * k + c):P * (4 * k + c + 1)],
                                                    g_ident)
                            last.then_inc(g_wt_ps, 1)
                            after(pe, g_wt_ok, 8 * n + k + 1)
                            for c in range(4):
                                last = pe.matmul(ps_s[:, 0:F], g_wt[:, P * c:P * (c + 1)], rhs[:, 4 * k + c, :],
                                                 start=(k == 0 and c == 0), stop=(k == 7 and c == 3))
                            last.then_inc(g_prod, 1)
                        if phase == 1:
                            after(pe, g_hn, t + 2)
                            pe.transpose(ps_f[:, 0:P], g_ht[:, 0:P], g_ident).then_inc(g_turned, 1)
                            after(pe, g_t_ok, NB + t + 1)
                            pe.matmul(ps_t[:, 1, 0:F], g_ht[:, P:2 * P], g_wm, start=True, stop=True).then_inc(g_f, 1)

        @block.vector
        def _(dve):
            links = [0]

            def chain(ins):
                links[0] += 1
                ins.then_inc(v, 1)
                dve.wait_ge(v, links[0])

            dve.sem_inc(ev_used, 1)
            dve.sem_inc(side_used, 2)
            dve.sem_inc(sums_used, 2)
            for h in range(2):
                dve.sem_inc(out_done[h], 64)
                dve.sem_inc(feat_out[h], 16)
            dve.memset(ones_col[:, :], 1.0)

            def edges(p, q, half):
                n = 2 * q + half
                dve.wait_ge(adj_in[n], 64 * (p + 1))
                dve.tensor_scalar(edge[:, q, 2 * JQ * half:2 * JQ * (half + 1)], adj_ring[:, n, :], 1.0,
                                  float(POS[q] | NEG[q]), ALU.is_ge, ALU.mult).then_inc(edge_ok, 1)

            def turned(b):
                dve.wait_ge(turned_ok, b + 1)
                if b >= 2:
                    dve.wait_ge(f_ok, b - 1)
                dve.tensor_copy(h_t[:, b % 2], ps_t[:, b % 2]).then_inc(h_t_ok, 1)

            for b in range(NB):
                if b % 2 == 0:
                    dve.wait_ge(x_in[b // 2], 64)
                for t in range(E4 * b, E4 * (b + 1)):
                    ins = dve.bn_stats(stats[:, t, :], x_all[:, t, :])
                chain(ins)
                for t in range(E4 * b, E4 * (b + 1)):
                    ins = dve.bn_aggr(mv[:, t, :], stats[:, t, :])
                chain(ins)
                dve.tensor_scalar(nmean[:, E4 * b:E4 * (b + 1)], mv[:, E4 * b:E4 * (b + 1), 0], -1.0, None, ALU.mult)\
                    .then_inc(mean_ok, 1)
                if b >= 2:
                    turned(b - 2)
            dve.tensor_scalar(tmp[:, 0], mv[:, :, 1], EPS, None, ALU.add).then_inc(var_ok, 1)
            turned(NB - 2)
            dve.wait_ge(const_ok, 8)
            for q in range(QUAD):
                ins = dve.tensor_reduce(lanes[:, q, :], ident.rearrange("p (a c) -> p c a", a=QUAD), AX.X, ALU.add)
            chain(ins)
            turned(NB - 1)
            dve.wait_ge(root_ok, 1)
            chain(dve.reciprocal(tmp[:, 2], tmp[:, 1]))
            chain(dve.tensor_tensor(tmp[:, 3], tmp[:, 0], tmp[:, 2], ALU.mult))
            chain(dve.tensor_tensor(tmp[:, 4], tmp[:, 1], tmp[:, 3], ALU.add))
            chain(dve.tensor_scalar(tmp[:, 5], tmp[:, 4], 0.5, None, ALU.mult))
            chain(dve.reciprocal(rstd[:, :], tmp[:, 5]))
            dve.tensor_tensor(nmr[:, :], nmean, rstd[:, :], ALU.mult)
            dve.wait_ge(f_ok, NB)
            chain(dve.tensor_tensor(fj, ps_f[:, 0:2 * T].rearrange("p (t k) -> p k t", k=2),
                                    rstd[:, None, :].broadcast_to([P, 2, T]), ALU.mult))
            dve.tensor_reduce(ext[:, 0:1], fj[:, 1, :], AX.X, ALU.max)
            chain(dve.tensor_reduce(ext[:, 1:2], fj[:, 1, :], AX.X, ALU.min))
            dve.tensor_tensor(ext_rows, ext[:, 0:2][:, :, None].broadcast_to([P, 2, P]),
                              ident[:, None, :].broadcast_to([P, 2, P]), ALU.mult).then_inc(ext_ok, 1)
            dve.tensor_tensor(spread.rearrange("p (b r e) -> p b r e", b=NB, e=E4),
                              fj[:, 1, :].rearrange("p (b e) -> p b e", e=E4)[:, :, None, :].broadcast_to([P, NB, LANE, E4]),
                              lanes[:, 0, :][:, None, :, None].broadcast_to([P, NB, LANE, E4]),
                              ALU.mult).then_inc(spread_ok, 1)
            dve.tensor_tensor(f1_spread, fj[:, 0, :][:, None, :].broadcast_to([P, QUAD, T]),
                              quads[:, ::LANE][:, :, None].broadcast_to([P, QUAD, T]), ALU.mult).then_inc(spread_ok, 1)
            dve.wait_ge(ext_ps_ok, 1)
            dve.tensor_reduce(ext[:, 2:3], ps_f[:, P:2 * P], AX.X, ALU.max)
            chain(dve.tensor_reduce(ext[:, 3:4], ps_f[:, 2 * P:3 * P], AX.X, ALU.min))
            top = ext[:, 2:3]
            dve.tensor_scalar(wrong[:, 0:1], top, ext[:, 3:4], F2_RANGE, ALU.subtract, ALU.is_gt)
            chain(dve.tensor_scalar(tmp[:, 2], fj[:, 1], top, None, ALU.subtract))
            dve.tensor_scalar(tmp[:, 3], tmp[:, 2], SLOPE, None, ALU.mult).then_inc(arg_ok, 1)
            chain(dve.tensor_scalar(tmp[:, 6], fj[:, 0], top, None, ALU.add))
            dve.scalar_tensor_tensor(out=tmp[:, 7], in0=tmp[:, 6], scalar=SLOPE, in1=tmp[:, 6],
                                     op0=ALU.mult, op1=ALU.max).then_inc(arg_ok, 1)
            dve.wait_ge(arg_ok, 2)
            dve.tensor_tensor(tmp[:, 4], tmp[:, 6], tmp[:, 7], ALU.subtract).then_inc(arg_ok, 1)
            dve.scalar_tensor_tensor(out=tmp[:, 5], in0=tmp[:, 6], scalar=SLOPE, in1=tmp[:, 7],
                                     op0=ALU.mult, op1=ALU.subtract).then_inc(arg_ok, 1)
            for half in range(2):
                edges(0, 0, half)
            dve.wait_ge(f2_ps_ok, 3)
            dve.tensor_copy(f1_rep[:, :, :], ps_s[:, 0:P].rearrange("p (g t) -> p g t", g=QUAD)).then_inc(f1_ok, 1)
            dve.wait_ge(f1_ok, 1)
            dve.tensor_scalar(minus_f1[:, :, :], f1_rep[:, 2:4, :], -1.0, None, ALU.mult).then_inc(f1_ok, 1)
            dve.wait_ge(temp_ok, 1)
            chain(dve.tensor_scalar(coe[:, :], coe[:, :], 1.0, None, ALU.add))
            chain(dve.reciprocal(coe[:, :], coe[:, :]))
            one_less, minus_c3, one_less_c1, c0_rest, h0_share = (cmix[:, n:n + 1] for n in range(5))
            dve.tensor_scalar(one_less, coe[:, 2:3], -1.0, 1.0, ALU.mult, ALU.add)
            dve.tensor_scalar(minus_c3, coe[:, 3:4], -1.0, None, ALU.mult)
            dve.tensor_scalar(h0_share, coe[:, 0:1], -1.0, 1.0, ALU.mult, ALU.add)
            chain(dve.tensor_scalar(one_less_c1, coe[:, 1:2], -1.0, 1.0, ALU.mult, ALU.add))
            dve.tensor_tensor(c0_rest, one_less_c1, coe[:, 0:1], ALU.mult)
            dve.tensor_tensor(h0_share, one_less_c1, h0_share, ALU.mult)
            dve.wait_ge(exp_ok, 2)
            chain(dve.tensor_scalar(bdh[:, :, :], bd[:, :, :], S_H, None, ALU.mult))
            chain(dve.tensor_tensor(bdx, bdh[:, :, :], rstd[:, None, :].broadcast_to([P, 2, T]), ALU.mult))

            def scale_rows(b):
                if b >= 2:
                    dve.wait_ge(low_ok, b - 1)
                for k in range(2):
                    dve.tensor_tensor(scaled[:, 2 * (b % 2) + k].rearrange("p (e f) -> p e f", e=E4),
                                      h_all[:, E4 * b:E4 * (b + 1), :],
                                      bdx[:, k, E4 * b:E4 * (b + 1)][:, :, None].broadcast_to([P, E4, F]),
                                      ALU.mult).then_inc(scaled_ok, 1)

            def low_rows(b):
                dve.wait_ge(high_ok, 2 * b + 2)
                for k, dst in enumerate((xb, xd)):
                    ins = dve.tensor_tensor(dst[:, E4 * b:E4 * (b + 1), LO:LO + F],
                                            scaled[:, 2 * (b % 2) + k].rearrange("p (e f) -> p e f", e=E4),
                                            dst[:, E4 * b:E4 * (b + 1), 0:F], ALU.subtract)
                ins.then_inc(low_ok, 1)

            chain(dve.tensor_tensor(tmp[:, 0:2], bd[:, :, :], bd[:, :, :], ALU.mult))
            chain(dve.tensor_scalar(tmp[:, 2:4], tmp[:, 0:2], S_SQ, None, ALU.mult))
            for k, dst in enumerate((xb, xd)):
                dve.tensor_copy(dst[:, :, F:F + 1], bdh[:, k, :][:, :, None])
                chain(dve.tensor_copy(dst[:, :, F + 1:F + 2], tmp[:, 2 + k][:, :, None]))
                dve.tensor_tensor(dst[:, :, LO + F:LO + F + 1], bdh[:, k, :][:, :, None], dst[:, :, F:F + 1], ALU.subtract)
                dve.tensor_tensor(dst[:, :, LO + F + 1:LO + F + 2], tmp[:, 2 + k][:, :, None], dst[:, :, F + 1:F + 2],
                                  ALU.subtract)
                dve.memset(dst[:, :, CNT:CNT + 2], 1.0)
            chain(dve.tensor_tensor(tmp[:, 0:2], ac[:, :, :], ac[:, :, :], ALU.mult))
            for k, vals in enumerate((POS_VAL, NEG_VAL)):
                for q in range(2):
                    dve.tensor_scalar(ac1[:, k, q::2], ac[:, k, q::2], 1.0 / (S_H * vals[q]), None, ALU.mult)
                    dve.tensor_scalar(acsq[:, k, q::2], tmp[:, k, q::2], 1.0 / (S_SQ * vals[q]), None, ALU.mult)
            dve.tensor_scalar(bdf[:, :, :], bd[:, :, :], S_F, None, ALU.mult).then_inc(ready_ok, 1)

            def encode(p, first=False):
                for q in range(2):
                    dve.wait_ge(side_ok, 2 * p + q + 1)
                    dve.wait_ge(edge_ok, 4 * p + 2 * q + 2)
                    dve.wait_ge(pool_side_ok, 2 * p + q + 2)
                    dve.scalar_tensor_tensor(out=edge[:, q, :].bitcast(I32), in0=side[:, q, :].bitcast(I32),
                                             scalar=word(POS[q]), in1=edge[:, q, :].bitcast(I32),
                                             op0=ALU.bitwise_xor, op1=ALU.bitwise_and).then_inc(side_used, 1)
                dve.wait_ge(side_used, 2 * p + 4)
                dve.tensor_tensor(edge[:, 0, :].bitcast(I32), edge[:, 0, :].bitcast(I32), edge[:, 1, :].bitcast(I32),
                                  ALU.bitwise_or).then_inc(merged, 1)
                dve.wait_ge(merged, p + 1)
                if not first:
                    dve.wait_ge(flags_ok, 8 * p)
                    dve.wait_ge(saved, p)
                dve.transpose(both_t[:, :, :].rearrange("p b (g c) -> p g b c", g=QUAD),
                              edge[:, 0, :].bitcast(I32).rearrange("p (g b r) -> p g b r", g=QUAD, b=NB))\
                    .then_inc(both_ok, 1)

            def flags_of(src, n, q, halves=(0, 1)):
                for half in halves:
                    for k, bit in enumerate((POS[q], NEG[q])):
                        s = 4 * q + 2 * half + k
                        dve.wait_ge(flags_used, 8 * n + s + 1)
                        dve.tensor_scalar(flags[:, s % RING], src[:, 4 * half:4 * half + 4, :], word(bit), None,
                                          ALU.bitwise_and).then_inc(flags_ok, 1)

            def steps(sem_, base):
                at = [0]

                def step(ins):
                    at[0] += 1
                    ins.then_inc(sem_, 1)

                def settle():
                    dve.wait_ge(sem_, base + at[0])
                return step, settle, at

            def pair_feat(i, h, meanwhile=lambda k: None):
                p = 2 * i + h
                pair = bass.ds(4 * i + 2 * h, 2)
                one = [bass.ds(4 * i + 2 * h + q, 1) for q in range(2)]
                step, settle, at = steps(step1, STEPS1 * p)
                for q in range(2):
                    dve.wait_ge(sums_used, 2 * p + q + 3)
                    step(dve.tensor_scalar(acc[:, q, :], ev[:, q, 0, 0:2 * LO], ac1[:, 0, one[q]], None, ALU.mult))
                step(dve.tensor_tensor(small[:, 0, :].rearrange("p (q k) -> p q k", q=2), ev[:, :, :, F + 1],
                                       ev[:, :, :, LO + F + 1], ALU.add))
                step(dve.tensor_copy(cnt[:, pair, :], ev[:, :, :, CNT]))
                meanwhile(0)
                settle()
                for q in range(2):
                    step(dve.scalar_tensor_tensor(out=acc[:, q, :], in0=ev[:, q, 1, 0:2 * LO], scalar=ac1[:, 1, one[q]],
                                                  in1=acc[:, q, :], op0=ALU.mult, op1=ALU.add))
                step(dve.tensor_tensor(small[:, 1, :].rearrange("p (q k) -> p q k", q=2),
                                       small[:, 0, :].rearrange("p (q k) -> p q k", q=2),
                                       acsq[:, :, pair].rearrange("p k q -> p q k"), ALU.mult))
                meanwhile(1)
                settle()
                dve.tensor_tensor(num[:, :, :], acc[:, :, 0:F + 1], acc[:, :, LO:LO + F + 1], ALU.add).then_inc(ev_used, 1)
                step(dve.tensor_tensor(small[:, 2, 0:2], small[:, 1, 0:4:2], small[:, 1, 1:4:2], ALU.add))
                dve.wait_ge(ev_used, p + 2)
                step(dve.tensor_scalar(small[:, 3, 2:4], num[:, :, F], 1e-6, None, ALU.max))
                meanwhile(2)
                settle()
                step(dve.reciprocal(rden[:, pair], small[:, 3, 2:4]))
                settle()
                step(dve.tensor_tensor(small[:, 3, 0:2], small[:, 2, 0:2], rden[:, pair], ALU.mult))
                meanwhile(3)
                settle()
                step(dve.scalar_tensor_tensor(out=rs[:, pair], in0=small[:, 3, 0:2], scalar=0.5, in1=rden[:, pair],
                                              op0=ALU.mult, op1=ALU.mult))
                settle()
                step(dve.tensor_scalar(small[:, 4, 0:2], rs[:, pair], -1.0, one_less, ALU.mult, ALU.add))
                meanwhile(4)
                settle()
                dve.wait_ge(h_ok, p + 1)
                for q in range(2):
                    ins = dve.tensor_scalar(rows[:, h, q, :], rows[:, h, q, :], small[:, 4, q:q + 1], None, ALU.mult)
                step(ins)
                settle()
                dve.wait_ge(feat_out[h], 16 * (i + 1))
                for q in range(2):
                    ins = dve.scalar_tensor_tensor(out=feat[:, h, q, :], in0=num[:, q, 0:F], scalar=rden[:, one[q]],
                                                   in1=rows[:, h, q, :], op0=ALU.mult, op1=ALU.add)
                ins.then_inc(row_used, 1)
                dve.wait_ge(row_used, p + 1)
                step(dve.tensor_scalar(acc[:, :, 0:F], feat[:, h], THRESH, -THRESH, ALU.min, ALU.max))
                settle()
                dve.tensor_tensor(feat[:, h], feat[:, h], acc[:, :, 0:F], ALU.subtract).then_inc(feat_ok, 1)
                assert at[0] == STEPS1, at

            def low(i, h):
                dve.wait_ge(feat_ok, 2 * i + h + 1)
                dve.wait_ge(hi_ok, 2 * i + h + 1)
                for q in range(2):
                    t = bass.ds(4 * i + 2 * h + q, 1)
                    for k, dst in enumerate((fb, fd)):
                        ins = dve.scalar_tensor_tensor(out=dst[:, t, F:2 * F], in0=feat[:, h, q:q + 1, :], scalar=bdf[:, k, t],
                                                       in1=dst[:, t, 0:F], op0=ALU.mult, op1=ALU.subtract)
                ins.then_inc(feats_ok, 1)

            def turn(p, i, h):
                for half in range(2):
                    edges(p + 1, 0, half)

                def meanwhile(k):
                    if k in (0, 3):
                        edges(p + 1, 1, k // 3)
                    elif k in (1, 4):
                        flags_of(both_t, p, 1, (k // 3,))
                pair_feat(i, h, meanwhile)
                encode(p + 1)
                dve.wait_ge(both_ok, p + 2)
                flags_of(both_t, p + 1, 0)
                low(i, h)

            scale_rows(0)
            for b in range(NB):
                if b + 1 < NB:
                    scale_rows(b + 1)
                low_rows(b)
                if b < 2:
                    edges(0, 1, b)
                if b == 2:
                    encode(0, first=True)
                    dve.wait_ge(both_ok, 1)
                    flags_of(both_t, 0, 0)
            for half in range(2):
                flags_of(both_t, 0, 1, (half,))
                for n in range(2):
                    edges(1, half, n)
            encode(1)
            dve.wait_ge(both_ok, 2)
            flags_of(both_t, 1, 0)
            with dve.Fori(0, NB - 1) as i:
                turn(2 * i + 1, i, 0)
                turn(2 * i + 2, i, 1)

            def last_flags(k):
                if k in (1, 4):
                    flags_of(both_t, PAIRS - 1, 1, (k // 3,))
            pair_feat(NB - 1, 0, last_flags)
            dve.wait_ge(saved, PAIRS)
            flags_of(codes[:, 0], PAIRS, 0)
            low(NB - 1, 0)
            pair_feat(NB - 1, 1)
            low(NB - 1, 1)
            flags_of(codes[:, 0], PAIRS, 1)
            dve.scalar_tensor_tensor(out=ac2[:, :, :], in0=ac1[:, :, :], scalar=S_H / S_F,
                                     in1=rden[:, None, :].broadcast_to([P, 2, T]), op0=ALU.mult, op1=ALU.mult)
            chain(dve.tensor_scalar(wmix[:, :], rs[:, :], coe[:, 1:2], c0_rest, ALU.mult, ALU.add))
            dve.wait_ge(count_ok, 2 * T + 1)
            for q in range(2):
                chain(dve.tensor_scalar(rows_n[:, q::2], cnt[:, q::2, 0], 1.0 / POS_VAL[q], None, ALU.mult))
                chain(dve.scalar_tensor_tensor(out=rows_n[:, q::2], in0=cnt[:, q::2, 1], scalar=1.0 / NEG_VAL[q],
                                               in1=rows_n[:, q::2], op0=ALU.mult, op1=ALU.add))
            dve.tensor_reduce(wrong[:, 1:2], nz[:, :], AX.X, ALU.add)
            chain(dve.tensor_reduce(wrong[:, 2:3], rows_n[:, :], AX.X, ALU.add))
            chain(dve.tensor_tensor(wrong[:, 1:2], wrong[:, 1:2], wrong[:, 2:3], ALU.subtract))
            chain(dve.tensor_scalar(rows_n[:, :], rows_n[:, :], 0.0, None, ALU.is_equal))
            chain(dve.tensor_reduce(wrong[:, 2:3], rows_n[:, :], AX.X, ALU.add))
            chain(dve.tensor_tensor(wrong[:, 1:2], wrong[:, 1:2], wrong[:, 2:3], ALU.add))
            dve.tensor_tensor(wrong[:, 3:4], wrong[:, 0:1], wrong[:, 1:2], ALU.add).then_inc(wrong_ok, 1)

            def pair_out(i, h):
                p = 2 * i + h
                one = [bass.ds(4 * i + 2 * h + q, 1) for q in range(2)]
                step, settle, at = steps(step2, STEPS2 * p)
                dve.wait_ge(aux_in[h], 144 * (i + 1))
                step(dve.scalar_tensor_tensor(out=x_rows[:, h], in0=h0_rows[:, h], scalar=h0_share, in1=x_rows[:, h],
                                              op0=ALU.mult, op1=ALU.add))
                for q in range(2):
                    dve.wait_ge(sums_used, 2 * (PAIRS + p) + q + 3)
                    step(dve.tensor_scalar(acc[:, q, 0:W2], ev[:, q, 0, 0:W2], ac2[:, 0, one[q]], None, ALU.mult))
                settle()
                for q in range(2):
                    ins = dve.scalar_tensor_tensor(out=acc[:, q, 0:W2], in0=ev[:, q, 1, 0:W2], scalar=ac2[:, 1, one[q]],
                                                   in1=acc[:, q, 0:W2], op0=ALU.mult, op1=ALU.add)
                ins.then_inc(ev_used, 1)
                dve.wait_ge(ev_used, PAIRS + p + 2)
                step(dve.tensor_tensor(num[:, :, 0:F], acc[:, :, 0:F], acc[:, :, F:2 * F], ALU.add))
                settle()
                step(dve.scalar_tensor_tensor(out=feat_rows[:, h], in0=num[:, :, 0:F], scalar=minus_c3, in1=feat_rows[:, h],
                                              op0=ALU.mult, op1=ALU.add))
                step(dve.scalar_tensor_tensor(out=x_rows[:, h], in0=num[:, :, 0:F], scalar=coe[:, 1:2], in1=x_rows[:, h],
                                              op0=ALU.mult, op1=ALU.add))
                settle()
                dve.wait_ge(out_done[h], 64 * i + 64)
                for q in range(2):
                    ins = dve.scalar_tensor_tensor(out=y_rows[:, h, q], in0=feat_rows[:, h, q], scalar=wmix[:, one[q]],
                                                   in1=x_rows[:, h, q], op0=ALU.mult, op1=ALU.add)
                ins.then_inc(y_ok, 1)
                assert at[0] == STEPS2, at

            def front2(p, i, h):
                src = codes[:, bass.ds(p, 1)].rearrange("p o b i -> p (o b) i")
                flags_of(src, PAIRS + p, 0)
                pair_out(i, h)
                flags_of(src, PAIRS + p, 1)

            with dve.Fori(0, NB - 1) as i:
                front2(2 * i + 1, i, 0)
                front2(2 * i + 2, i, 1)
            front2(PAIRS - 1, NB - 1, 0)
            pair_out(NB - 1, 1)
            dve.wait_ge(wrong_ps_ok, 1)
            chain(dve.tensor_scalar(wrong[0:1, 0:1], ps_s[0:1, 0:1], 0.5, None, ALU.is_gt))
            dve.tensor_copy(flag_i[:, :], wrong[0:1, 0:1]).then_inc(flag_ok, 1)

            def root_refined(var, root, scratch, inv):
                chain_g(dve.reciprocal(scratch, root))
                chain_g(dve.tensor_tensor(scratch, var, scratch, ALU.mult))
                chain_g(dve.tensor_tensor(scratch, root, scratch, ALU.add))
                chain_g(dve.tensor_scalar(scratch, scratch, 0.5, None, ALU.mult))
                chain_g(dve.reciprocal(inv, scratch))

            def chain_g(ins):
                dve.drain()

            def g_product(n):
                for k in range(8):
                    after(dve, g_wt_ps, 8 * n + k + 1)
                    dve.tensor_copy(g_wt, ps_t[:, 0]).then_inc(g_wt_ok, 1)
                after(dve, g_prod, 8 * n + 8)

            def g_softmax(n, t):
                after(dve, g_adj_in, 16 * (n + 1))
                chain_g(dve.tensor_scalar(g_w, g_f2, g_f1[:, bass.ds(t, 1)], None, ALU.add))
                chain_g(dve.scalar_tensor_tensor(out=g_w, in0=g_w, scalar=SLOPE, in1=g_w, op0=ALU.mult, op1=ALU.max))
                chain_g(dve.tensor_scalar(g_t, g_adj, 0.0, -NEG_INF, ALU.is_gt, ALU.mult))
                chain_g(dve.scalar_tensor_tensor(out=g_w, in0=g_t, scalar=NEG_INF, in1=g_w, op0=ALU.add, op1=ALU.add))
                chain_g(dve.tensor_reduce(g_s[:, 0:1], g_w, AX.X, ALU.max))
                dve.tensor_scalar(g_s[:, 1:2], g_s[:, 0:1], -1.0, None, ALU.mult).then_inc(g_scored, 1)
                after(dve, g_exp, n + 1)
                chain_g(dve.reciprocal(g_s[:, 3:4], g_s[:, 2:3]))
                dve.tensor_scalar(g_w, g_w, g_s[:, 3:4], None, ALU.mult).then_inc(g_w_ok, 1)

            with general(dve):
                dve.wait_ge(g_in, 80)
                dve.memset(g_s[:, 5:6], -1.0)
                for t in range(T):
                    ins = dve.bn_stats(g_st[:, t, :], g_x[:, t, :])
                chain_g(ins)
                for t in range(T):
                    ins = dve.bn_aggr(g_mv[:, t, :], g_st[:, t, :])
                chain_g(ins)
                dve.tensor_scalar(g_tmp[:, 0], g_mv[:, :, 1], EPS, None, ALU.add).then_inc(g_var, 1)
                dve.wait_ge(g_root, 1)
                root_refined(g_tmp[:, 0], g_tmp[:, 1], g_tmp[:, 2], g_tmp[:, 3])
                for t in range(T):
                    ins = dve.tensor_scalar(g_h[:, t, :], g_x[:, t, :], g_mv[:, t, 0:1], g_tmp[:, 3, t:t + 1],
                                            ALU.subtract, ALU.mult)
                chain_g(ins)
                dve.tensor_scalar(g_h, g_h, 0.0, None, ALU.max)
                dve.tensor_copy(g_a2, g_a12[:, 1:2].broadcast_to([P, P])).then_inc(g_hn, 1)
                for b in range(NB):
                    dve.wait_ge(g_turned, b + 1)
                    dve.tensor_copy(g_ht, ps_t[:, 0]).then_inc(g_t_ok, 1)
                    dve.wait_ge(g_f, b + 1)
                    chain_g(dve.tensor_copy(g_f2[:, 512 * b:512 * (b + 1)], ps_t[:, 1]))
                chain_g(dve.tensor_copy(g_f1, ps_f[:, 0:T]))

                with dve.Fori(0, T) as t:
                    one = bass.ds(t, 1)
                    g_softmax(t, t)
                    g_product(t)
                    after(dve, g_sq, t + 1)
                    chain_g(dve.tensor_scalar(g_rs[:, one], g_s[:, 4:5], 0.5, None, ALU.mult))
                    chain_g(dve.tensor_scalar(g_s[:, 8:9], g_rs[:, one], -1.0, one_less, ALU.mult, ALU.add))
                    chain_g(dve.scalar_tensor_tensor(out=g_feat[:, one, :], in0=g_h[:, one, :], scalar=g_s[:, 8:9],
                                                     in1=ps_s[:, None, 0:F], op0=ALU.mult, op1=ALU.add))
                    chain_g(dve.tensor_scalar(g_wt[:, 0:F], g_feat[:, one, :].rearrange("p o f -> p (o f)"), THRESH, -THRESH,
                                              ALU.min, ALU.max))
                    chain_g(dve.tensor_tensor(g_feat[:, one, :], g_feat[:, one, :], g_wt[:, None, 0:F], ALU.subtract))

                with dve.Fori(0, T) as t:
                    one = bass.ds(t, 1)
                    g_softmax(T + t, t)
                    g_product(T + t)
                    after(dve, g_sq, T + t + 1)
                    pu, odd = ps_s[:, None, 0:F], g_wt[:, None, 0:F]
                    chain_g(dve.scalar_tensor_tensor(out=g_x[:, one, :], in0=g_h0[:, one, :], scalar=h0_share,
                                                     in1=g_x[:, one, :], op0=ALU.mult, op1=ALU.add))
                    chain_g(dve.scalar_tensor_tensor(out=odd, in0=pu, scalar=minus_c3, in1=g_feat[:, one, :],
                                                     op0=ALU.mult, op1=ALU.add))
                    chain_g(dve.scalar_tensor_tensor(out=g_x[:, one, :], in0=pu, scalar=coe[:, 1:2], in1=g_x[:, one, :],
                                                     op0=ALU.mult, op1=ALU.add))
                    chain_g(dve.tensor_scalar(g_s[:, 8:9], g_rs[:, one], coe[:, 1:2], c0_rest, ALU.mult, ALU.add))
                    chain_g(dve.scalar_tensor_tensor(out=g_x[:, one, :], in0=odd, scalar=g_s[:, 8:9], in1=g_x[:, one, :],
                                                     op0=ALU.mult, op1=ALU.add))
                    chain_g(dve.tensor_copy(g_ht[:, 0:F], g_x[:, one, :].rearrange("p o f -> p (o f)")))
                    chain_g(dve.bn_stats(g_st[:, 0, :], g_ht[:, 0:F]))
                    chain_g(dve.bn_aggr(g_mv[:, 0, :], g_st[:, 0, :]))
                    dve.tensor_scalar(g_s[:, 6:7], g_mv[:, 0, 1:2], EPS, None, ALU.add).then_inc(g_var, 1)
                    after(dve, g_root, t + 2)
                    root_refined(g_s[:, 6:7], g_s[:, 7:8], g_s[:, 8:9], g_s[:, 9:10])
                    chain_g(dve.tensor_scalar(g_ht[:, 0:F], g_ht[:, 0:F], g_mv[:, 0, 0:1], g_s[:, 9:10],
                                              ALU.subtract, ALU.mult))
                    dve.tensor_scalar(g_ht[:, 0:F], g_ht[:, 0:F], 0.0, None, ALU.max).then_inc(g_hn, 1)
                    after(dve, g_turned, NB + t + 1)
                    dve.tensor_copy(g_ht[:, P:2 * P], ps_f[:, 0:P]).then_inc(g_t_ok, 1)
                    after(dve, g_f, NB + t + 1)
                    chain_g(dve.tensor_tensor(g_msg[:, one, :], ps_t[:, 1, 0:F][:, None, :], g_bm[:, None, :], ALU.add))

                with dve.Fori(0, T) as t:
                    one = bass.ds(t, 1)
                    n = 2 * T + t
                    after(dve, g_adj_in, 16 * (n + 1))
                    chain_g(dve.tensor_tensor(g_t, g_adj, g_adj, ALU.mult))
                    chain_g(dve.tensor_scalar(g_t, g_t, 1e-4, 0.02, ALU.is_lt, ALU.mult))
                    chain_g(dve.tensor_tensor(g_w, g_t, g_adj, ALU.add))
                    dve.reciprocal(g_w, g_w).then_inc(g_scored, 1)
                    after(dve, g_exp, n + 1)
                    dve.scalar_tensor_tensor(out=g_w, in0=g_adj, scalar=1.0, in1=g_w, op0=ALU.is_lt,
                                             op1=ALU.mult).then_inc(g_w_ok, 1)
                    g_product(n)
                    chain_g(dve.tensor_tensor(g_x[:, one, :], ps_s[:, None, 0:F], g_x[:, one, :], ALU.add))
                dve.sem_inc(g_done, 1)


_INS = ['x', 'adj', 'L0_gnn_h0', 'L0_gnn_a', 'L0_gnn_temp', 'L1_gnn_W', 'L1_gnn_B']


def kernel(**inputs):
    import numpy as _np
    import concourse.bacc as _bacc
    from concourse import mybir as _mybir
    from concourse.bass_utils import run_bass_kernel_spmd as _run

    nc = _bacc.Bacc("TRN2", target_bir_lowering=False, num_devices=1)
    arrays, args = {}, []
    for name in _INS:
        a = _np.ascontiguousarray(inputs[name])
        arrays[f"in_{name}_dram"] = a
        args.append(nc.dram_tensor(f"in_{name}_dram", a.shape, _mybir.dt.from_np(a.dtype), kind="ExternalInput").ap())
    out = nc.dram_tensor("out_dram", (4096, 128), _mybir.dt.float32, kind="ExternalOutput").ap()
    build(nc, *args, out)
    r = _run(nc, [arrays], core_ids=[0])
    return r.results[0]["out_dram"]
```

```python
import concourse.bass as bass
from concourse import mybir
from contextlib import ExitStack

FP32, FP16, FP8 = mybir.dt.float32, mybir.dt.float16, mybir.dt.float8e4
U8, I8, I32, U32 = mybir.dt.uint8, mybir.dt.int8, mybir.dt.int32, mybir.dt.uint32
ALU, ACT, AX = mybir.AluOpType, mybir.ActivationFunctionType, mybir.AxisListType

P = 128
N, F = 4096, 128
T = N // P
PAIRS = T // 2
QUAD = 4
LANE = P // QUAD
JQ = N // QUAD
NB = JQ // P
E4 = 4
SLOPE, EPS, THRESH, NEG_INF = 0.2, 1e-5, 1e-6, -9e15
F2_RANGE = 10.0

S_H = 4096.0
S_SQ = 32768.0
S_F = 2048.0
CNT = F + 2
S1 = F + 3
LO = F + 4
W1 = 2 * LO
W2 = 2 * F

POS = (0x40, 0x10)
NEG = (0x20, 0x08)
POS_VAL = (2.0, 2.0 ** -5)
NEG_VAL = (2.0 ** -3, 2.0 ** -6)

RING = 4
STEPS1 = 13
STEPS2 = 6


def word(byte):
    return int(byte) * 0x01010101


def build(nc, x, adj, h0, a, temp, w_msg, b_msg, out):
    feat_scratch = nc.dram_tensor("feat_scratch", (PAIRS, P, 2 * F), FP32).ap()
    h_scratch = nc.dram_tensor("h_scratch", (PAIRS, P, 2 * F), FP32).ap()
    ctx = ExitStack()
    with ctx:
        def sb(name, shape, dt):
            return ctx.enter_context(nc.sbuf_tensor(name, shape, dt))

        def sem(name):
            return ctx.enter_context(nc.semaphore(name))

        codes = sb("codes", [P, PAIRS, NB, P], I32)
        xb = sb("xb", [P, T, W1], FP16)
        xd = sb("xd", [P, T, W1], FP16)
        fb = sb("fb", [P, T, W2], FP16)
        fd = sb("fd", [P, T, W2], FP16)
        adj_ring = sb("adj_ring", [P, 4, 2 * JQ], FP32)
        edge = sb("edge", [P, 2, N], U8)
        side = sb("side", [P, 2, N], I8)
        both_t = sb("both_t", [P, NB, P], I32)
        flags = sb("flags", [P, RING, 4, P], I32)
        f2_all = sb("f2_all", [P, JQ], FP32)
        f1_rep = sb("f1_rep", [P, QUAD, T], FP32)
        nz = sb("nz", [P, T], FP32)
        cnt = sb("cnt", [P, T, 2], FP32)
        ac = sb("ac", [P, 2, T], FP32)
        ac1 = sb("ac1", [P, 2, T], FP32)
        ac2 = sb("ac2", [P, 2, T], FP32)
        rden = sb("rden", [P, T], FP32)
        rs = sb("rs", [P, T], FP32)
        wmix = sb("wmix", [P, T], FP32)
        bd = sb("bd", [P, 2, T], FP32)
        bdh = sb("bdh", [P, 2, T], FP32)
        bdf = sb("bdf", [P, 2, T], FP32)
        rstd = sb("rstd", [P, T], FP32)
        coe = sb("coe", [P, 5], FP32)
        cmix = sb("cmix", [P, 6], FP32)
        small = sb("small", [P, 5, 4], FP32)
        acsq = sb("acsq", [P, 2, T], FP32)
        ones_col = sb("ones_col", [P, 1], FP32)
        wrong = sb("wrong", [P, 4], FP32)
        rows_n = sb("rows_n", [P, T], FP32)
        flag_i = sb("flag_i", [1, 1], I32)
        rows = sb("rows", [P, 2, 2, F], FP32)
        ev = sb("ev", [P, 2, 2, W2], FP32)
        acc = sb("acc", [P, 2, W2], FP32)
        num = sb("num", [P, 2, F + 1], FP32)
        feat = sb("feat", [P, 2, 2, F], FP32)

        early = codes[:, PAIRS // 2:, :, :].bitcast(FP32).rearrange("p s b i -> p (s b i)")
        x_all = early[:, 0:T * F].rearrange("p (t f) -> p t f", f=F)
        h_all = early[:, T * F:2 * T * F].rearrange("p (t f) -> p t f", f=F)
        scrap = fb[:, :, :].rearrange("p t w -> p (t w)").bitcast(FP32)
        h_t = scrap[:, 0:1024].rearrange("p (s w) -> p s w", s=2)
        spread = scrap[:, 1024:2048]
        scaled = scrap[:, 2048:4096].rearrange("p (s w) -> p s w", s=4)
        scrap2 = fd[:, :, :].rearrange("p t w -> p (t w)").bitcast(FP32)
        ident = scrap2[:, 0:128]
        quads = scrap2[:, 128:256]
        lanes = scrap2[:, 256:384].rearrange("p (a c) -> p a c", a=QUAD)
        ones = scrap2[:, 384:512]
        f1_spread = scrap2[:, 512:640].rearrange("p (g t) -> p g t", g=QUAD)
        stats = scrap2[:, 640:640 + 6 * T].rearrange("p (t s) -> p t s", s=6)
        mv = scrap2[:, 1024:1024 + 2 * T].rearrange("p (t s) -> p t s", s=2)
        a12 = scrap2[:, 1100:1102]
        fj = scrap2[:, 1104:1104 + 2 * T].rearrange("p (k t) -> p k t", k=2)
        tmp = scrap2[:, 1200:1200 + 8 * T].rearrange("p (n t) -> p n t", t=T)
        nmean = scrap2[:, 1460:1460 + T]
        ext = scrap2[:, 1500:1504]
        ext_rows = scrap2[:, 1600:1600 + 2 * P].rearrange("p (k c) -> p k c", k=2)
        bdx = scrap2[:, 1900:1900 + 2 * T].rearrange("p (k t) -> p k t", k=2)

        g_rows = codes[:, :, :, :].bitcast(FP32).rearrange("p s b i -> p (s b i)")
        g_f2, g_x, g_h0, g_msg = (g_rows[:, N * n:N * (n + 1)] for n in range(4))
        g_x, g_h0, g_msg = (w.rearrange("p (t f) -> p t f", f=F) for w in (g_x, g_h0, g_msg))
        g_h = scrap.rearrange("p (t f) -> p t f", f=F)
        g_feat = scrap2.rearrange("p (t f) -> p t f", f=F)
        g_adj = adj_ring[:, 0:2, :].rearrange("p s j -> p (s j)")
        g_w = xb[:, :, :].rearrange("p t w -> p (t w)").bitcast(FP32)[:, 0:N]
        g_t = xd[:, :, :].rearrange("p t w -> p (t w)").bitcast(FP32)[:, 0:N]
        g_more = adj_ring[:, 2:4, :].rearrange("p s j -> p (s j)")
        g_wt, g_ident, g_wm, g_bm, g_a2, g_ht = (g_more[:, 512 * n:512 * n + w] for n, w in
                                                 enumerate((512, P, F, F, P, 512)))
        g_st = g_more[:, 3072:3072 + 6 * T].rearrange("p (t s) -> p t s", s=6)
        g_mv = g_more[:, 3328:3328 + 2 * T].rearrange("p (t s) -> p t s", s=2)
        g_tmp = g_more[:, 3400:3400 + 5 * T].rearrange("p (n t) -> p n t", t=T)
        g_f1 = g_more[:, 3600:3600 + T]
        g_rs = g_more[:, 3640:3640 + T]
        g_a12 = g_more[:, 3680:3682]
        g_s = g_more[:, 3700:3712]

        ps = ctx.enter_context(nc.psum_tensor("ps", [P, 2, 2, 512], FP32))
        ps_more = ctx.enter_context(nc.psum_tensor("ps_more", [P, 4, 512], FP32))
        ps_t, ps_f, ps_s = ps_more[:, 0:2], ps_more[:, 2], ps_more[:, 3]

        x_in = [sem(f"x_in{c}") for c in range(NB // 2)]
        a_in = sem("a_in")
        adj_in = [sem(f"adj_in{s}") for s in range(4)]
        h_out = sem("h_out")
        row_in = [sem(f"row_in{s}") for s in range(2)]
        aux_in = [sem(f"aux_in{s}") for s in range(2)]
        feat_out = [sem(f"feat_out{s}") for s in range(2)]
        out_done = [sem(f"out_done{s}") for s in range(2)]
        const_ok = sem("const_ok")
        v = sem("v")
        var_ok = sem("var_ok")
        root_ok = sem("root_ok")
        mean_ok = sem("mean_ok")
        h_chunk_ok = sem("h_chunk_ok")
        turned_ok = sem("turned_ok")
        h_t_ok = sem("h_t_ok")
        f_ok = sem("f_ok")
        spread_ok = sem("spread_ok")
        f2_ps_ok = sem("f2_ps_ok")
        f2_ok = sem("f2_ok")
        f1_ok = sem("f1_ok")
        ext_ok = sem("ext_ok")
        ext_ps_ok = sem("ext_ps_ok")
        arg_ok = sem("arg_ok")
        exp_ok = sem("exp_ok")
        temp_ok = sem("temp_ok")
        scaled_ok = sem("scaled_ok")
        high_ok = sem("high_ok")
        low_ok = sem("low_ok")
        ready_ok = sem("ready_ok")
        edge_ok = sem("edge_ok")
        count_ok = sem("count_ok")
        side_ok = sem("side_ok")
        side_used = sem("side_used")
        merged = sem("merged")
        both_ok = sem("both_ok")
        saved = sem("saved")
        flags_ok = sem("flags_ok")
        turn = sem("turn")
        flags_used = sem("flags_used")
        sums_used = sem("sums_used")
        ev_used = sem("ev_used")
        row_used = sem("row_used")
        step1 = sem("step1")
        feat_ok = sem("feat_ok")
        hi_ok = sem("hi_ok")
        feats_ok = sem("feats_ok")
        step2 = sem("step2")
        y_ok = sem("y_ok")
        wrong_ok = sem("wrong_ok")
        wrong_ps_ok = sem("wrong_ps_ok")
        flag_ok = sem("flag_ok")
        going_on = sem("going_on")
        g_in = sem("g_in")
        g_adj_in = sem("g_adj_in")
        g_const = sem("g_const")
        g_seen = sem("g_seen")
        g_root = sem("g_root")
        g_var = sem("g_var")
        g_hn = sem("g_hn")
        g_turned = sem("g_turned")
        g_t_ok = sem("g_t_ok")
        g_f = sem("g_f")
        g_scored = sem("g_scored")
        g_exp = sem("g_exp")
        g_w_ok = sem("g_w_ok")
        g_sq = sem("g_sq")
        g_wt_ps = sem("g_wt_ps")
        g_wt_ok = sem("g_wt_ok")
        g_prod = sem("g_prod")
        g_done = sem("g_done")
        g_out = sem("g_out")
        block = ctx.enter_context(nc.Block())

        def after(eng, sem_, value):
            eng.wait_ge(sem_, value)
            eng.sem_inc(g_seen, 1)

        def general(eng):
            eng.wait_ge(flag_ok, 1)
            return eng.If(eng.value_load(flag_i[0:1, 0:1], min_val=0, max_val=1) == 1)

        adj_v = adj.rearrange("(g b c e) (a j) -> a b e c g j", g=QUAD, b=NB, c=LANE, e=E4, a=QUAD)
        x_v = x.rearrange("(g b c e) f -> g b c (e f)", g=QUAD, b=NB, c=LANE, e=E4)
        h0_v = h0.rearrange("(g b c e) f -> g b c (e f)", g=QUAD, b=NB, c=LANE, e=E4)
        out_v = out.rearrange("(g b c e) f -> g b c (e f)", g=QUAD, b=NB, c=LANE, e=E4)

        aux = adj_ring[:, :, :].rearrange("p s j -> p (s j)")
        h0_rows, x_rows, feat_rows, y_rows = (
            aux[:, 512 * n:512 * (n + 1)].rearrange("p (s e f) -> p s e f", s=2, e=2) for n in range(4))

        def pair_rows(view, b, h, g):
            return view[g, b, :, 2 * F * h:2 * F * (h + 1)]

        def lanes_of(tile, g):
            return tile[LANE * g:LANE * (g + 1)].rearrange("c e f -> c (e f)")

        @block.sync
        def _(sp):
            def load_adj(b, e, half, slot):
                for q in range(QUAD):
                    sp.dma_start(adj_ring[LANE * q:LANE * (q + 1), slot, :].rearrange("c (g j) -> c g j", g=2),
                                 adj_v[q, b, e, :, 2 * half:2 * half + 2, :]).then_inc(adj_in[slot], 16)

            def slot_free(t, half):
                sp.wait_ge(edge_ok, 2 * t + half + 1)
                sp.sem_inc(going_on, 1)
                sp.wait_ge(count_ok, t + 1)
                sp.sem_inc(going_on, 1)

            for b in range(0, NB, 2):
                for g in range(QUAD):
                    sp.dma_start(x_all[LANE * g:LANE * (g + 1), E4 * b:E4 * (b + 2), :]
                                 .rearrange("c (b e) f -> c b (e f)", b=2),
                                 x_v[g, b:b + 2].rearrange("b c w -> c b w")).then_inc(x_in[b // 2], 16)

            def load_rows(b, h):
                sp.dma_start(rows[:, h].rearrange("p e f -> p (e f)"),
                             h_scratch[bass.ds(2 * b + h, 1)].rearrange("o p w -> (o p) w")).then_inc(row_in[h], 16)

            def store_feat(b, h):
                sp.wait_ge(feat_ok, 2 * b + h + 1)
                sp.sem_inc(going_on, 1)
                sp.dma_start(feat_scratch[bass.ds(2 * b + h, 1)].rearrange("o p w -> (o p) w"),
                             feat[:, h].rearrange("p e f -> p (e f)")).then_inc(feat_out[h], 16)

            def load_half(b, h, q, half, first=False):
                if not first:
                    slot_free(2 * (2 * b + h) - 2 + q, half)
                load_adj(b, 2 * h + q, half, 2 * q + half)

            def load_rest(b, h):
                for q, half in ((0, 1), (1, 0), (1, 1)):
                    load_half(b, h, q, half)

            def turn_rows(b, h):
                store_feat(b, h)
                sp.wait_ge(row_used, 2 * b + h + 1)
                sp.sem_inc(going_on, 1)
                load_rows(b + 1, h)

            for q in range(2):
                for half in range(2):
                    load_half(0, 0, q, half, first=True)
            sp.wait_ge(h_chunk_ok, NB)
            sp.dma_start(h_scratch.rearrange("s p w -> p s w"), h_all.rearrange("p (s e) f -> p s (e f)", e=2))\
                .then_inc(h_out, 16)
            sp.wait_ge(h_out, 16)
            for h in range(2):
                load_rows(0, h)
            load_half(0, 1, 0, 0)
            for b, h in ((0, 1), (1, 0)):
                load_rest(b, h)
                load_half(b + h, 1 - h, 0, 0)
            with sp.Fori(0, NB - 2) as b:
                for h in range(2):
                    load_rest(b + 1 + h, 1 - h)
                    load_half(b + 2, h, 0, 0)
                    turn_rows(b, h)
            load_rest(NB - 1, 1)
            for h in range(2):
                turn_rows(NB - 2, h)
            for h in range(2):
                store_feat(NB - 1, h)

            def load_aux(b, h):
                for g in range(QUAD):
                    sp.dma_start(lanes_of(h0_rows[:, h], g), pair_rows(h0_v, b, h, g)).then_inc(aux_in[h], 16)
                    sp.dma_start(lanes_of(x_rows[:, h], g), pair_rows(x_v, b, h, g)).then_inc(aux_in[h], 16)
                sp.dma_start(feat_rows[:, h].rearrange("p e f -> p (e f)"),
                             feat_scratch[bass.ds(2 * b + h, 1)].rearrange("o p w -> (o p) w")).then_inc(aux_in[h], 16)

            def store_out(b, h):
                sp.wait_ge(y_ok, 2 * b + h + 1)
                for g in range(QUAD):
                    sp.dma_start(pair_rows(out_v, b, h, g), lanes_of(y_rows[:, h], g)).then_inc(out_done[h], 16)

            slot_free(T - 1, 1)
            for s in range(2):
                sp.wait_ge(feat_out[s], 16 * (PAIRS // 2 + 1))
            load_aux(0, 0)
            load_aux(0, 1)
            with sp.Fori(0, NB - 1) as b:
                for h in range(2):
                    store_out(b, h)
                    load_aux(b + 1, h)
            for h in range(2):
                store_out(NB - 1, h)
            for s in range(2):
                sp.wait_ge(out_done[s], 64 * (NB + 1))

            with general(sp):
                rows_of = lambda m: m.rearrange("(t p) f -> p t f", p=P)
                sp.dma_start(g_x, rows_of(x)).then_inc(g_in, 16)
                sp.dma_start(g_h0, rows_of(h0)).then_inc(g_in, 16)
                sp.dma_start(g_wm, w_msg).then_inc(g_in, 16)
                sp.dma_start(g_bm, b_msg.rearrange("(o f) -> o f", o=1).broadcast_to([P, F])).then_inc(g_in, 16)
                sp.dma_start(g_a12, a.rearrange("(k f) o -> f (k o)", k=2), allow_slow_non_contiguous=True)\
                    .then_inc(g_in, 16)
                adj_rows = adj.rearrange("(t p) j -> t p j", p=P)
                for phase in range(3):
                    if phase:
                        sp.wait_ge(g_w_ok, T * phase)
                    sp.dma_start(g_adj, adj_rows[0]).then_inc(g_adj_in, 16)
                    with sp.Fori(0, T - 1) as t:
                        sp.wait_ge(g_w_ok, T * phase + t + 1)
                        sp.dma_start(g_adj, adj_rows[bass.ds(t + 1, 1)].rearrange("o p j -> (o p) j")).then_inc(g_adj_in, 16)
                sp.wait_ge(g_done, 1)
                sp.dma_start(rows_of(out), g_x).then_inc(g_out, 16)
                sp.wait_ge(g_out, 16)

        @block.gpsimd
        def _(pool):
            pool.memset(ident, 0.0).then_inc(const_ok, 1)
            pool.memset(quads, 0.0).then_inc(const_ok, 1)
            pool.memset(ones, 1.0).then_inc(const_ok, 1)
            pool.wait_ge(const_ok, 3)
            pool.affine_select(out=ident, in_=ident, compare_op=ALU.not_equal, fill=1.0, base=0,
                               pattern=[[-1, P]], channel_multiplier=1).then_inc(const_ok, 1)
            for q in range(QUAD):
                pool.wait_ge(const_ok, 4 + q)
                pool.memset(quads[LANE * q:LANE * (q + 1), LANE * q:LANE * (q + 1)], 1.0).then_inc(const_ok, 1)

            with general(pool):
                pool.memset(g_ident, 0.0).then_inc(g_const, 1)
                pool.wait_ge(g_const, 1)
                pool.affine_select(out=g_ident, in_=g_ident, compare_op=ALU.not_equal, fill=1.0, base=0,
                                   pattern=[[-1, P]], channel_multiplier=1).then_inc(g_const, 1)

        @block.scalar
        def _(act):
            act.dma_start(a12, a.rearrange("(k f) o -> f (k o)", k=2), allow_slow_non_contiguous=True).then_inc(a_in, 16)
            act.dma_start(coe[:, :], temp.rearrange("(o k) -> o k", o=1).broadcast_to([P, 5])).then_inc(a_in, 16)
            for b in range(NB):
                act.wait_ge(mean_ok, b + 1)
                for t in range(E4 * b, E4 * (b + 1)):
                    last = act.activation(h_all[:, t, :], x_all[:, t, :], ACT.Relu, bias=nmean[:, t:t + 1])
                last.then_inc(h_chunk_ok, 1)
            act.wait_ge(var_ok, 1)
            act.activation(tmp[:, 1], tmp[:, 0], ACT.Sqrt).then_inc(root_ok, 1)

            def save(p):
                act.wait_ge(both_ok, p + 1)
                act.sem_inc(going_on, 1)
                act.dma_start(codes[:, bass.ds(p, 1), :, :], both_t[:, None, :, :]).then_inc(saved, 16)

            def count(p, q):
                act.wait_ge(side_used, 2 * p + q + 1)
                for half in range(2):
                    act.wait_ge(adj_in[2 * q + half], 64 * (p + 1))
                act.activation(side[:, q, :], adj_ring[:, 2 * q:2 * q + 2, :].rearrange("p s j -> p (s j)").bitcast(U32),
                               ACT.Sign, accum_out=nz[:, bass.ds(2 * p + q, 1)]).then_inc(count_ok, 1)

            def compare(p, q, groups=(0, 1, 2, 3)):
                if 0 in groups:
                    act.wait_ge(count_ok, 2 * p + q + 1)
                for g in groups:
                    last = act.activation(side[:, q, JQ * g:JQ * (g + 1)], f2_all[:, :], ACT.Sign,
                                          bias=f1_rep[:, g, bass.ds(2 * p + q, 1)])
                    if g == QUAD - 1:
                        last.then_inc(side_ok, 1)

            def drain(p, q, width):
                act.wait_ge(flags_used, 4 * (2 * p + q + 1) + RING)
                act.wait_ge(ev_used, p + 1)
                act.activation(ev[:, q, :, 0:width], ps[:, q, :, 0:width], ACT.Copy).then_inc(sums_used, 1)

            def high(i, h):
                act.wait_ge(feat_ok, 2 * i + h + 1)
                for q in range(2):
                    t = bass.ds(4 * i + 2 * h + q, 1)
                    for k, dst in enumerate((fb, fd)):
                        last = act.activation(dst[:, t, 0:F], feat[:, h, q:q + 1, :], ACT.Copy, scale=bdf[:, k, t])
                last.then_inc(hi_ok, 1)

            def turn(p, i, h, after_next=True):
                count(p + 1, 1)
                save(p)
                drain(p - 1, 1, S1)
                compare(p + 1, 1)
                if after_next:
                    count(p + 2, 0)
                drain(p, 0, S1)
                if after_next:
                    compare(p + 2, 0)
                high(i, h)

            for q in range(2):
                count(0, q)
            act.wait_ge(arg_ok, 4)
            act.activation(bd[:, :, :], tmp[:, 2:4], ACT.Exp).then_inc(exp_ok, 1)
            act.activation(ac[:, :, :], tmp[:, 4:6], ACT.Exp).then_inc(exp_ok, 1)
            for n in range(2):
                act.wait_ge(f2_ps_ok, n + 1)
                act.activation(f2_all[:, 512 * n:512 * (n + 1)], ps_t[:, n], ACT.Copy).then_inc(f2_ok, 1)
            act.wait_ge(a_in, 32)
            act.activation(coe[:, :], coe[:, :], ACT.Exp, scale=-1.0).then_inc(temp_ok, 1)
            act.wait_ge(f1_ok, 1)
            act.wait_ge(f2_ok, 2)

            def meanwhile(b):
                if b == 0:
                    compare(0, 0, (0, 1, 2))
                elif b == 1:
                    compare(0, 0, (3,))
                    compare(0, 1, (0, 1))
                elif b == 2:
                    compare(0, 1, (2, 3))
                elif b == 4:
                    count(1, 0)
                    save(0)
                elif b in (5, 6):
                    compare(1, 0, (2 * b - 10, 2 * b - 9))
                elif b == 7:
                    count(1, 1)

            for b in range(NB):
                for k, dst in enumerate((xb, xd)):
                    act.wait_ge(scaled_ok, 2 * b + k + 1)
                    act.activation(dst[:, E4 * b:E4 * (b + 1), 0:F],
                                   scaled[:, 2 * (b % 2) + k].rearrange("p (e f) -> p e f", e=E4),
                                   ACT.Copy).then_inc(high_ok, 1)
                meanwhile(b)
            compare(1, 1)
            count(2, 0)
            drain(0, 0, S1)
            compare(2, 0)
            with act.Fori(0, NB - 2) as i:
                turn(2 * i + 1, i, 0)
                turn(2 * i + 2, i, 1)
            turn(PAIRS - 3, NB - 2, 0)
            turn(PAIRS - 2, NB - 2, 1, after_next=False)
            save(PAIRS - 1)
            drain(PAIRS - 2, 1, S1)
            drain(PAIRS - 1, 0, S1)
            high(NB - 1, 0)
            drain(PAIRS - 1, 1, S1)
            high(NB - 1, 1)
            with act.Fori(PAIRS, 2 * PAIRS) as p:
                for q in range(2):
                    drain(p, q, W2)

            with general(act):
                act.wait_ge(g_var, 1)
                act.activation(g_tmp[:, 1], g_tmp[:, 0], ACT.Sqrt).then_inc(g_root, 1)
                for phase in range(3):
                    with act.Fori(0, T) as t:
                        n = T * phase + t
                        after(act, g_scored, n + 1)
                        if phase < 2:
                            act.activation(g_w, g_w, ACT.Exp, bias=g_s[:, 1:2], accum_out=g_s[:, 2:3]).then_inc(g_exp, 1)
                            after(act, g_w_ok, n + 1)
                            act.activation(g_t, g_w, ACT.Square, accum_out=g_s[:, 4:5]).then_inc(g_sq, 1)
                        else:
                            act.activation(g_t, g_w, ACT.Square, bias=g_s[:, 5:6]).then_inc(g_sq, 1)
                            after(act, g_sq, n + 1)
                            act.activation(g_w, g_t, ACT.Exp, scale=-2.0).then_inc(g_exp, 1)
                        if phase == 1:
                            after(act, g_var, t + 2)
                            act.activation(g_s[:, 7:8], g_s[:, 6:7], ACT.Sqrt).then_inc(g_root, 1)

        @block.tensor
        def _(pe):
            pe.sem_inc(flags_used, RING)
            pe.wait_ge(const_ok, 8)
            pe.wait_ge(a_in, 32)

            def project(b):
                pe.wait_ge(h_t_ok, b + 1)
                for e in range(E4):
                    last = pe.matmul(ps_f[:, 2 * (E4 * b + e):2 * (E4 * b + e) + 2], h_t[:, b % 2, P * e:P * (e + 1)], a12,
                                     start=True, stop=True)
                last.then_inc(f_ok, 1)

            for b in range(NB):
                pe.wait_ge(h_chunk_ok, b + 1)
                if b >= 2:
                    pe.wait_ge(h_t_ok, b - 1)
                for e in range(E4):
                    last = pe.transpose(ps_t[:, b % 2, P * e:P * (e + 1)], h_all[:, E4 * b + e, :], ident)
                last.then_inc(turned_ok, 1)
                if b >= 1:
                    project(b - 1)
            project(NB - 1)
            pe.wait_ge(ext_ok, 1)
            pe.matmul(ps_f[:, P:3 * P], ones, ext_rows.rearrange("p k c -> p (k c)"), start=True, stop=True)\
                .then_inc(ext_ps_ok, 1)
            pe.wait_ge(spread_ok, 2)
            for n in range(2):
                pe.matmul(ps_t[:, n], quads, spread[:, 512 * n:512 * (n + 1)], start=True, stop=True).then_inc(f2_ps_ok, 1)
            pe.matmul(ps_s[:, 0:P], lanes.rearrange("p a c -> p (a c)"), f1_spread.rearrange("p g t -> p (g t)"),
                      start=True, stop=True).then_inc(f2_ps_ok, 1)

            def tile_sums(p, q, ops, parts, gate=None, late=T):
                pe.wait_ge(sums_used, 2 * p + q + 1)
                for half in range(2):
                    tiles = range(T // 2 * half, T // 2 * (half + 1))
                    for k, t in [(k, t) for last_ones in (False, True) for k in range(2) for t in tiles
                                 if (t >= late) == last_ones]:
                        s = 4 * q + 2 * half + k
                        if t == tiles[0]:
                            pe.wait_ge(flags_ok, 8 * p + s + 1)
                            pe.sem_inc(turn, 1)
                        if k == 0 and gate is not None:
                            gate(t)
                        bytes_ = flags[:, s % RING].bitcast(FP8).rearrange("p b (i e) -> p b i e", e=E4)
                        for n, (at, width) in enumerate(parts):
                            last = pe.matmul(ps[:, q, k, 0:width], bytes_[:, t // E4 - 4 * half, :, t % E4],
                                             ops[k][:, t, at:at + width], start=(t == 0 and n == 0),
                                             stop=(t == T - 1 and n == len(parts) - 1))
                        if t == tiles[-1]:
                            last.then_inc(flags_used, 1)

            def rows_there(t):
                if t % E4 == 0:
                    pe.wait_ge(low_ok, t // E4 + 1)

            pe.wait_ge(ready_ok, 1)
            high_low = ((0, S1), (LO, S1))
            tile_sums(0, 0, (xb, xd), high_low, rows_there)
            tile_sums(0, 1, (xb, xd), high_low)
            with pe.Fori(1, PAIRS) as p:
                for q in range(2):
                    tile_sums(p, q, (xb, xd), high_low)

            def feats_there(t):
                if t % 8 == 0 or t == T - 2:
                    pe.wait_ge(feats_ok, min(t // 2 + 4, PAIRS - 1) if t < T - 2 else PAIRS)

            tile_sums(PAIRS, 0, (fb, fd), ((0, W2),), feats_there, late=T - 2)
            tile_sums(PAIRS, 1, (fb, fd), ((0, W2),))
            with pe.Fori(PAIRS + 1, 2 * PAIRS) as p:
                for q in range(2):
                    tile_sums(p, q, (fb, fd), ((0, W2),))
            pe.wait_ge(wrong_ok, 1)
            pe.matmul(ps_s[0:1, 0:1], wrong[:, 3:4], ones_col[:, :], start=True, stop=True).then_inc(wrong_ps_ok, 1)

            with general(pe):
                pe.wait_ge(g_const, 2)
                for b in range(NB):
                    if b == 0:
                        pe.wait_ge(g_hn, 1)
                    for e in range(E4):
                        last = pe.transpose(ps_t[:, 0, P * e:P * (e + 1)], g_h[:, E4 * b + e, :], g_ident)
                    last.then_inc(g_turned, 1)
                    pe.wait_ge(g_t_ok, b + 1)
                    for e in range(E4):
                        pe.matmul(ps_f[:, E4 * b + e:E4 * b + e + 1], g_ht[:, P * e:P * (e + 1)], g_a12[:, 0:1],
                                  start=True, stop=True)
                    pe.matmul(ps_t[:, 1], g_a2, g_ht, start=True, stop=True).then_inc(g_f, 1)
                for phase, rhs in enumerate((g_h, g_feat, g_msg)):
                    with pe.Fori(0, T) as t:
                        n = T * phase + t
                        after(pe, g_w_ok, n + 1)
                        for k in range(8):
                            for c in range(4):
                                last = pe.transpose(ps_t[:, 0, P * c:P * (c + 1)], g_w[:, P * (4 * k + c):P * (4 * k + c + 1)],
                                                    g_ident)
                            last.then_inc(g_wt_ps, 1)
                            after(pe, g_wt_ok, 8 * n + k + 1)
                            for c in range(4):
                                last = pe.matmul(ps_s[:, 0:F], g_wt[:, P * c:P * (c + 1)], rhs[:, 4 * k + c, :],
                                                 start=(k == 0 and c == 0), stop=(k == 7 and c == 3))
                            last.then_inc(g_prod, 1)
                        if phase == 1:
                            after(pe, g_hn, t + 2)
                            pe.transpose(ps_f[:, 0:P], g_ht[:, 0:P], g_ident).then_inc(g_turned, 1)
                            after(pe, g_t_ok, NB + t + 1)
                            pe.matmul(ps_t[:, 1, 0:F], g_ht[:, P:2 * P], g_wm, start=True, stop=True).then_inc(g_f, 1)

        @block.vector
        def _(dve):
            links = [0]

            def chain(ins):
                links[0] += 1
                ins.then_inc(v, 1)
                dve.wait_ge(v, links[0])

            dve.sem_inc(ev_used, 1)
            dve.sem_inc(side_used, 2)
            dve.sem_inc(sums_used, 2)
            for h in range(2):
                dve.sem_inc(out_done[h], 64)
                dve.sem_inc(feat_out[h], 16)
            dve.memset(ones_col[:, :], 1.0)

            def edges(p, q, half, first=False):
                n = 2 * q + half
                if not first:
                    dve.wait_ge((merged, both_ok)[q], p)
                dve.wait_ge(adj_in[n], 64 * (p + 1))
                dve.tensor_scalar(edge[:, q, 2 * JQ * half:2 * JQ * (half + 1)], adj_ring[:, n, :], 1.0,
                                  float(POS[q] | NEG[q]), ALU.is_ge, ALU.mult).then_inc(edge_ok, 1)

            def turned(b):
                dve.wait_ge(turned_ok, b + 1)
                if b >= 2:
                    dve.wait_ge(f_ok, b - 1)
                dve.tensor_copy(h_t[:, b % 2], ps_t[:, b % 2]).then_inc(h_t_ok, 1)

            dve.wait_ge(const_ok, 8)
            for q in range(QUAD):
                ins = dve.tensor_reduce(lanes[:, q, :], ident.rearrange("p (a c) -> p c a", a=QUAD), AX.X, ALU.add)
            chain(ins)
            for b in range(NB):
                if b % 2 == 0:
                    dve.wait_ge(x_in[b // 2], 64)
                for t in range(E4 * b, E4 * (b + 1)):
                    ins = dve.bn_stats(stats[:, t, :], x_all[:, t, :])
                chain(ins)
                for t in range(E4 * b, E4 * (b + 1)):
                    ins = dve.bn_aggr(mv[:, t, :], stats[:, t, :])
                chain(ins)
                dve.tensor_scalar(nmean[:, E4 * b:E4 * (b + 1)], mv[:, E4 * b:E4 * (b + 1), 0], -1.0, None, ALU.mult)\
                    .then_inc(mean_ok, 1)
                if b >= 2:
                    turned(b - 2)
            dve.tensor_scalar(tmp[:, 0], mv[:, :, 1], EPS, None, ALU.add).then_inc(var_ok, 1)
            turned(NB - 2)
            dve.wait_ge(root_ok, 1)
            chain(dve.reciprocal(tmp[:, 2], tmp[:, 1]))
            chain(dve.tensor_tensor(tmp[:, 3], tmp[:, 0], tmp[:, 2], ALU.mult))
            chain(dve.tensor_tensor(tmp[:, 4], tmp[:, 1], tmp[:, 3], ALU.add))
            chain(dve.tensor_scalar(tmp[:, 5], tmp[:, 4], 0.5, None, ALU.mult))
            chain(dve.reciprocal(rstd[:, :], tmp[:, 5]))
            turned(NB - 1)
            for half in range(2):
                edges(0, 0, half, first=True)
            dve.wait_ge(f_ok, NB)
            chain(dve.tensor_tensor(fj, ps_f[:, 0:2 * T].rearrange("p (t k) -> p k t", k=2),
                                    rstd[:, None, :].broadcast_to([P, 2, T]), ALU.mult))
            dve.tensor_reduce(ext[:, 0:1], fj[:, 1, :], AX.X, ALU.max)
            chain(dve.tensor_reduce(ext[:, 1:2], fj[:, 1, :], AX.X, ALU.min))
            dve.tensor_tensor(ext_rows, ext[:, 0:2][:, :, None].broadcast_to([P, 2, P]),
                              ident[:, None, :].broadcast_to([P, 2, P]), ALU.mult).then_inc(ext_ok, 1)
            dve.tensor_tensor(spread.rearrange("p (b r e) -> p b r e", b=NB, e=E4),
                              fj[:, 1, :].rearrange("p (b e) -> p b e", e=E4)[:, :, None, :].broadcast_to([P, NB, LANE, E4]),
                              lanes[:, 0, :][:, None, :, None].broadcast_to([P, NB, LANE, E4]),
                              ALU.mult).then_inc(spread_ok, 1)
            dve.tensor_tensor(f1_spread, fj[:, 0, :][:, None, :].broadcast_to([P, QUAD, T]),
                              quads[:, ::LANE][:, :, None].broadcast_to([P, QUAD, T]), ALU.mult).then_inc(spread_ok, 1)
            dve.wait_ge(ext_ps_ok, 1)
            dve.tensor_reduce(ext[:, 2:3], ps_f[:, P:2 * P], AX.X, ALU.max)
            chain(dve.tensor_reduce(ext[:, 3:4], ps_f[:, 2 * P:3 * P], AX.X, ALU.min))
            top = ext[:, 2:3]
            dve.tensor_scalar(wrong[:, 0:1], top, ext[:, 3:4], F2_RANGE, ALU.subtract, ALU.is_gt)
            chain(dve.tensor_scalar(tmp[:, 2], fj[:, 1], top, None, ALU.subtract))
            dve.tensor_scalar(tmp[:, 3], tmp[:, 2], SLOPE, None, ALU.mult).then_inc(arg_ok, 1)
            chain(dve.tensor_scalar(tmp[:, 6], fj[:, 0], top, None, ALU.add))
            dve.scalar_tensor_tensor(out=tmp[:, 7], in0=tmp[:, 6], scalar=SLOPE, in1=tmp[:, 6],
                                     op0=ALU.mult, op1=ALU.max).then_inc(arg_ok, 1)
            dve.wait_ge(arg_ok, 2)
            dve.tensor_tensor(tmp[:, 4], tmp[:, 6], tmp[:, 7], ALU.subtract).then_inc(arg_ok, 1)
            dve.scalar_tensor_tensor(out=tmp[:, 5], in0=tmp[:, 6], scalar=SLOPE, in1=tmp[:, 7],
                                     op0=ALU.mult, op1=ALU.subtract).then_inc(arg_ok, 1)
            dve.wait_ge(exp_ok, 2)
            chain(dve.tensor_scalar(bdh[:, :, :], bd[:, :, :], S_H, None, ALU.mult))
            chain(dve.tensor_tensor(bdx, bdh[:, :, :], rstd[:, None, :].broadcast_to([P, 2, T]), ALU.mult))

            def scale_rows(b):
                if b >= 2:
                    dve.wait_ge(low_ok, b - 1)
                for k in range(2):
                    dve.tensor_tensor(scaled[:, 2 * (b % 2) + k].rearrange("p (e f) -> p e f", e=E4),
                                      h_all[:, E4 * b:E4 * (b + 1), :],
                                      bdx[:, k, E4 * b:E4 * (b + 1)][:, :, None].broadcast_to([P, E4, F]),
                                      ALU.mult).then_inc(scaled_ok, 1)

            def low_rows(b):
                dve.wait_ge(high_ok, 2 * b + 2)
                for k, dst in enumerate((xb, xd)):
                    ins = dve.tensor_tensor(dst[:, E4 * b:E4 * (b + 1), LO:LO + F],
                                            scaled[:, 2 * (b % 2) + k].rearrange("p (e f) -> p e f", e=E4),
                                            dst[:, E4 * b:E4 * (b + 1), 0:F], ALU.subtract)
                ins.then_inc(low_ok, 1)

            chain(dve.tensor_tensor(tmp[:, 0:2], bd[:, :, :], bd[:, :, :], ALU.mult))
            chain(dve.tensor_scalar(tmp[:, 2:4], tmp[:, 0:2], S_SQ, None, ALU.mult))
            for k, dst in enumerate((xb, xd)):
                dve.tensor_copy(dst[:, :, F:F + 1], bdh[:, k, :][:, :, None])
                chain(dve.tensor_copy(dst[:, :, F + 1:F + 2], tmp[:, 2 + k][:, :, None]))
                dve.tensor_tensor(dst[:, :, LO + F:LO + F + 1], bdh[:, k, :][:, :, None], dst[:, :, F:F + 1], ALU.subtract)
                dve.tensor_tensor(dst[:, :, LO + F + 1:LO + F + 2], tmp[:, 2 + k][:, :, None], dst[:, :, F + 1:F + 2],
                                  ALU.subtract)
                dve.memset(dst[:, :, CNT:CNT + 1], 1.0)
                ins = dve.memset(dst[:, :, LO + CNT:LO + CNT + 1], 0.0)
            ins.then_inc(ready_ok, 1)

            def select(p, q):
                dve.wait_ge(side_ok, 2 * p + q + 1)
                dve.wait_ge(edge_ok, 4 * p + 2 * q + 2)
                dve.scalar_tensor_tensor(out=edge[:, q, :].bitcast(I32), in0=side[:, q, :].bitcast(I32),
                                         scalar=word(POS[q]), in1=edge[:, q, :].bitcast(I32),
                                         op0=ALU.bitwise_xor, op1=ALU.bitwise_and).then_inc(side_used, 1)

            def merge(p):
                dve.wait_ge(side_used, 2 * p + 4)
                dve.tensor_tensor(edge[:, 1, :].bitcast(I32), edge[:, 0, :].bitcast(I32), edge[:, 1, :].bitcast(I32),
                                  ALU.bitwise_or).then_inc(merged, 1)

            def transpose(p, first=False):
                dve.wait_ge(merged, p + 1)
                if not first:
                    dve.wait_ge(flags_ok, 8 * p)
                    dve.wait_ge(saved, 16 * p)
                dve.transpose(both_t[:, :, :].rearrange("p b (g c) -> p g b c", g=QUAD),
                              edge[:, 1, :].bitcast(I32).rearrange("p (g b r) -> p g b r", g=QUAD, b=NB))\
                    .then_inc(both_ok, 1)

            def flags_of(src, n, q, halves=(0, 1)):
                for half in halves:
                    for k, bit in enumerate((POS[q], NEG[q])):
                        s = 4 * q + 2 * half + k
                        dve.wait_ge(flags_used, 8 * n + s + 1)
                        dve.tensor_scalar(flags[:, s % RING], src[:, 4 * half:4 * half + 4, :], word(bit), None,
                                          ALU.bitwise_and).then_inc(flags_ok, 1)

            def steps(sem_, base):
                at = [0]

                def step(ins):
                    at[0] += 1
                    ins.then_inc(sem_, 1)

                def settle():
                    dve.wait_ge(sem_, base + at[0])
                return step, settle, at

            def pair_feat(i, h, meanwhile=lambda k: None):
                p = 2 * i + h
                pair = bass.ds(4 * i + 2 * h, 2)
                one = [bass.ds(4 * i + 2 * h + q, 1) for q in range(2)]
                step, settle, at = steps(step1, STEPS1 * p)
                for q in range(2):
                    dve.wait_ge(sums_used, 2 * p + q + 3)
                    step(dve.tensor_scalar(acc[:, q, 0:F + 1], ev[:, q, 0, 0:F + 1], ac1[:, 0, one[q]], None, ALU.mult))
                step(dve.tensor_tensor(small[:, 1, :].rearrange("p (q k) -> p q k", q=2), ev[:, :, :, F + 1],
                                       acsq[:, :, pair].rearrange("p k q -> p q k"), ALU.mult))
                step(dve.tensor_copy(cnt[:, pair, :], ev[:, :, :, CNT]))
                meanwhile(0)
                settle()
                for q in range(2):
                    ins = dve.scalar_tensor_tensor(out=num[:, q, :], in0=ev[:, q, 1, 0:F + 1], scalar=ac1[:, 1, one[q]],
                                                   in1=acc[:, q, 0:F + 1], op0=ALU.mult, op1=ALU.add)
                ins.then_inc(ev_used, 1)
                step(dve.tensor_tensor(small[:, 2, 0:2], small[:, 1, 0:4:2], small[:, 1, 1:4:2], ALU.add))
                meanwhile(1)
                dve.wait_ge(ev_used, p + 2)
                step(dve.tensor_scalar(small[:, 3, 2:4], num[:, :, F], 1e-6, None, ALU.max))
                meanwhile(2)
                settle()
                step(dve.reciprocal(rden[:, pair], small[:, 3, 2:4]))
                settle()
                step(dve.tensor_tensor(small[:, 3, 0:2], small[:, 2, 0:2], rden[:, pair], ALU.mult))
                meanwhile(3)
                settle()
                step(dve.scalar_tensor_tensor(out=rs[:, pair], in0=small[:, 3, 0:2], scalar=0.5, in1=rden[:, pair],
                                              op0=ALU.mult, op1=ALU.mult))
                settle()
                step(dve.tensor_scalar(small[:, 4, 0:2], rs[:, pair], -1.0, one_less, ALU.mult, ALU.add))
                meanwhile(4)
                settle()
                step(dve.tensor_tensor(small[:, 4, 2:4], small[:, 4, 0:2], rstd[:, pair], ALU.mult))
                settle()
                dve.wait_ge(row_in[h], 16 * (i + 1))
                for q in range(2):
                    ins = dve.tensor_scalar(rows[:, h, q, :], rows[:, h, q, :], small[:, 4, q + 2:q + 3], None, ALU.mult)
                step(ins)
                meanwhile(5)
                settle()
                dve.wait_ge(feat_out[h], 16 * (i + 1))
                for q in range(2):
                    ins = dve.scalar_tensor_tensor(out=feat[:, h, q, :], in0=num[:, q, 0:F], scalar=rden[:, one[q]],
                                                   in1=rows[:, h, q, :], op0=ALU.mult, op1=ALU.add)
                ins.then_inc(row_used, 1)
                dve.wait_ge(row_used, p + 1)
                step(dve.tensor_scalar(acc[:, :, 0:F], feat[:, h], THRESH, -THRESH, ALU.min, ALU.max))
                meanwhile(6)
                settle()
                dve.tensor_tensor(feat[:, h], feat[:, h], acc[:, :, 0:F], ALU.subtract).then_inc(feat_ok, 1)
                assert at[0] == STEPS1, at

            def low(i, h):
                dve.wait_ge(feat_ok, 2 * i + h + 1)
                dve.wait_ge(hi_ok, 2 * i + h + 1)
                for q in range(2):
                    t = bass.ds(4 * i + 2 * h + q, 1)
                    for k, dst in enumerate((fb, fd)):
                        ins = dve.scalar_tensor_tensor(out=dst[:, t, F:2 * F], in0=feat[:, h, q:q + 1, :], scalar=bdf[:, k, t],
                                                       in1=dst[:, t, 0:F], op0=ALU.mult, op1=ALU.subtract)
                ins.then_inc(feats_ok, 1)

            def operands(p, after_next=True):
                transpose(p)
                dve.wait_ge(both_ok, p + 1)
                flags_of(both_t, p, 0)
                if after_next:
                    edges(p + 1, 0, 1)

            def turn(p, i, h, after_next=True):
                def meanwhile(k):
                    if k in (0, 2):
                        edges(p + 1, 1, k // 2)
                    elif k in (1, 4):
                        flags_of(both_t, p, 1, (k // 3,))
                    elif k == 3:
                        select(p + 1, 1)
                    elif k == 5:
                        merge(p + 1)
                    elif after_next:
                        edges(p + 2, 0, 0)
                select(p + 1, 0)
                pair_feat(i, h, meanwhile)
                operands(p + 1, after_next)
                low(i, h)

            scale_rows(0)
            dve.wait_ge(f2_ps_ok, 3)
            dve.tensor_copy(f1_rep[:, :, :], ps_s[:, 0:P].rearrange("p (g t) -> p g t", g=QUAD)).then_inc(f1_ok, 1)
            for b in range(NB):
                if b + 1 < NB:
                    scale_rows(b + 1)
                low_rows(b)
                if b < 2:
                    edges(0, 1, b, first=True)
                if b == 2:
                    for q in range(2):
                        select(0, q)
                    merge(0)
                    transpose(0, first=True)
                    dve.wait_ge(both_ok, 1)
                    flags_of(both_t, 0, 0)
                if b in (4, 5):
                    edges(1, 0, b - 4)
                if b == 6:
                    flags_of(both_t, 0, 1, (0,))
            for half in range(2):
                edges(1, 1, half)
            chain(dve.tensor_tensor(tmp[:, 0:2], ac[:, :, :], ac[:, :, :], ALU.mult))
            for k, vals in enumerate((POS_VAL, NEG_VAL)):
                for q in range(2):
                    dve.tensor_scalar(ac1[:, k, q::2], ac[:, k, q::2], 1.0 / (S_H * vals[q]), None, ALU.mult)
                    dve.tensor_scalar(acsq[:, k, q::2], tmp[:, k, q::2], 1.0 / (S_SQ * vals[q]), None, ALU.mult)
            chain(dve.tensor_scalar(bdf[:, :, :], bd[:, :, :], S_F, None, ALU.mult))
            dve.wait_ge(temp_ok, 1)
            chain(dve.tensor_scalar(coe[:, :], coe[:, :], 1.0, None, ALU.add))
            chain(dve.reciprocal(coe[:, :], coe[:, :]))
            one_less, minus_c3, one_less_c1, c0_rest, h0_share = (cmix[:, n:n + 1] for n in range(5))
            dve.tensor_scalar(one_less, coe[:, 2:3], -1.0, 1.0, ALU.mult, ALU.add)
            dve.tensor_scalar(minus_c3, coe[:, 3:4], -1.0, None, ALU.mult)
            dve.tensor_scalar(h0_share, coe[:, 0:1], -1.0, 1.0, ALU.mult, ALU.add)
            chain(dve.tensor_scalar(one_less_c1, coe[:, 1:2], -1.0, 1.0, ALU.mult, ALU.add))
            dve.tensor_tensor(c0_rest, one_less_c1, coe[:, 0:1], ALU.mult)
            dve.tensor_tensor(h0_share, one_less_c1, h0_share, ALU.mult)
            flags_of(both_t, 0, 1, (1,))
            for q in range(2):
                select(1, q)
            merge(1)
            edges(2, 0, 0)
            operands(1)
            with dve.Fori(0, NB - 2) as i:
                turn(2 * i + 1, i, 0)
                turn(2 * i + 2, i, 1)
            turn(PAIRS - 3, NB - 2, 0)
            turn(PAIRS - 2, NB - 2, 1, after_next=False)

            def last_flags(k):
                if k in (1, 4):
                    flags_of(both_t, PAIRS - 1, 1, (k // 3,))
            pair_feat(NB - 1, 0, last_flags)
            dve.wait_ge(saved, 16 * PAIRS)
            flags_of(codes[:, 0], PAIRS, 0)
            low(NB - 1, 0)
            pair_feat(NB - 1, 1)
            low(NB - 1, 1)
            flags_of(codes[:, 0], PAIRS, 1)
            dve.scalar_tensor_tensor(out=ac2[:, :, :], in0=ac1[:, :, :], scalar=S_H / S_F,
                                     in1=rden[:, None, :].broadcast_to([P, 2, T]), op0=ALU.mult, op1=ALU.mult)
            chain(dve.tensor_scalar(wmix[:, :], rs[:, :], coe[:, 1:2], c0_rest, ALU.mult, ALU.add))
            dve.wait_ge(count_ok, T)
            for q in range(2):
                chain(dve.tensor_scalar(rows_n[:, q::2], cnt[:, q::2, 0], 1.0 / POS_VAL[q], None, ALU.mult))
                chain(dve.scalar_tensor_tensor(out=rows_n[:, q::2], in0=cnt[:, q::2, 1], scalar=1.0 / NEG_VAL[q],
                                               in1=rows_n[:, q::2], op0=ALU.mult, op1=ALU.add))
            dve.tensor_reduce(wrong[:, 1:2], nz[:, :], AX.X, ALU.add)
            chain(dve.tensor_reduce(wrong[:, 2:3], rows_n[:, :], AX.X, ALU.add))
            chain(dve.tensor_tensor(wrong[:, 1:2], wrong[:, 1:2], wrong[:, 2:3], ALU.subtract))
            chain(dve.tensor_scalar(rows_n[:, :], rows_n[:, :], 0.0, None, ALU.is_equal))
            chain(dve.tensor_reduce(wrong[:, 2:3], rows_n[:, :], AX.X, ALU.add))
            chain(dve.tensor_tensor(wrong[:, 1:2], wrong[:, 1:2], wrong[:, 2:3], ALU.add))
            dve.tensor_tensor(wrong[:, 3:4], wrong[:, 0:1], wrong[:, 1:2], ALU.add).then_inc(wrong_ok, 1)

            def pair_out(i, h):
                p = 2 * i + h
                one = [bass.ds(4 * i + 2 * h + q, 1) for q in range(2)]
                step, settle, at = steps(step2, STEPS2 * p)
                dve.wait_ge(aux_in[h], 144 * (i + 1))
                step(dve.scalar_tensor_tensor(out=x_rows[:, h], in0=h0_rows[:, h], scalar=h0_share, in1=x_rows[:, h],
                                              op0=ALU.mult, op1=ALU.add))
                for q in range(2):
                    dve.wait_ge(sums_used, 2 * (PAIRS + p) + q + 3)
                    step(dve.tensor_scalar(acc[:, q, 0:W2], ev[:, q, 0, 0:W2], ac2[:, 0, one[q]], None, ALU.mult))
                settle()
                for q in range(2):
                    ins = dve.scalar_tensor_tensor(out=acc[:, q, 0:W2], in0=ev[:, q, 1, 0:W2], scalar=ac2[:, 1, one[q]],
                                                   in1=acc[:, q, 0:W2], op0=ALU.mult, op1=ALU.add)
                ins.then_inc(ev_used, 1)
                dve.wait_ge(ev_used, PAIRS + p + 2)
                step(dve.tensor_tensor(num[:, :, 0:F], acc[:, :, 0:F], acc[:, :, F:2 * F], ALU.add))
                settle()
                step(dve.scalar_tensor_tensor(out=feat_rows[:, h], in0=num[:, :, 0:F], scalar=minus_c3, in1=feat_rows[:, h],
                                              op0=ALU.mult, op1=ALU.add))
                step(dve.scalar_tensor_tensor(out=x_rows[:, h], in0=num[:, :, 0:F], scalar=coe[:, 1:2], in1=x_rows[:, h],
                                              op0=ALU.mult, op1=ALU.add))
                settle()
                dve.wait_ge(out_done[h], 64 * i + 64)
                for q in range(2):
                    ins = dve.scalar_tensor_tensor(out=y_rows[:, h, q], in0=feat_rows[:, h, q], scalar=wmix[:, one[q]],
                                                   in1=x_rows[:, h, q], op0=ALU.mult, op1=ALU.add)
                ins.then_inc(y_ok, 1)
                assert at[0] == STEPS2, at

            def front2(p, i, h):
                src = codes[:, bass.ds(p, 1)].rearrange("p o b i -> p (o b) i")
                flags_of(src, PAIRS + p, 0)
                pair_out(i, h)
                flags_of(src, PAIRS + p, 1)

            with dve.Fori(0, NB - 1) as i:
                front2(2 * i + 1, i, 0)
                front2(2 * i + 2, i, 1)
            front2(PAIRS - 1, NB - 1, 0)
            pair_out(NB - 1, 1)
            dve.wait_ge(wrong_ps_ok, 1)
            chain(dve.tensor_scalar(wrong[0:1, 0:1], ps_s[0:1, 0:1], 0.5, None, ALU.is_gt))
            dve.tensor_copy(flag_i[:, :], wrong[0:1, 0:1]).then_inc(flag_ok, 1)

            def root_refined(var, root, scratch, inv):
                chain_g(dve.reciprocal(scratch, root))
                chain_g(dve.tensor_tensor(scratch, var, scratch, ALU.mult))
                chain_g(dve.tensor_tensor(scratch, root, scratch, ALU.add))
                chain_g(dve.tensor_scalar(scratch, scratch, 0.5, None, ALU.mult))
                chain_g(dve.reciprocal(inv, scratch))

            def chain_g(ins):
                dve.drain()

            def g_product(n):
                for k in range(8):
                    after(dve, g_wt_ps, 8 * n + k + 1)
                    dve.tensor_copy(g_wt, ps_t[:, 0]).then_inc(g_wt_ok, 1)
                after(dve, g_prod, 8 * n + 8)

            def g_softmax(n, t):
                after(dve, g_adj_in, 16 * (n + 1))
                chain_g(dve.tensor_scalar(g_w, g_f2, g_f1[:, bass.ds(t, 1)], None, ALU.add))
                chain_g(dve.scalar_tensor_tensor(out=g_w, in0=g_w, scalar=SLOPE, in1=g_w, op0=ALU.mult, op1=ALU.max))
                chain_g(dve.tensor_scalar(g_t, g_adj, 0.0, -NEG_INF, ALU.is_gt, ALU.mult))
                chain_g(dve.scalar_tensor_tensor(out=g_w, in0=g_t, scalar=NEG_INF, in1=g_w, op0=ALU.add, op1=ALU.add))
                chain_g(dve.tensor_reduce(g_s[:, 0:1], g_w, AX.X, ALU.max))
                dve.tensor_scalar(g_s[:, 1:2], g_s[:, 0:1], -1.0, None, ALU.mult).then_inc(g_scored, 1)
                after(dve, g_exp, n + 1)
                chain_g(dve.reciprocal(g_s[:, 3:4], g_s[:, 2:3]))
                dve.tensor_scalar(g_w, g_w, g_s[:, 3:4], None, ALU.mult).then_inc(g_w_ok, 1)

            with general(dve):
                dve.wait_ge(g_in, 80)
                dve.memset(g_s[:, 5:6], -1.0)
                for t in range(T):
                    ins = dve.bn_stats(g_st[:, t, :], g_x[:, t, :])
                chain_g(ins)
                for t in range(T):
                    ins = dve.bn_aggr(g_mv[:, t, :], g_st[:, t, :])
                chain_g(ins)
                dve.tensor_scalar(g_tmp[:, 0], g_mv[:, :, 1], EPS, None, ALU.add).then_inc(g_var, 1)
                dve.wait_ge(g_root, 1)
                root_refined(g_tmp[:, 0], g_tmp[:, 1], g_tmp[:, 2], g_tmp[:, 3])
                for t in range(T):
                    ins = dve.tensor_scalar(g_h[:, t, :], g_x[:, t, :], g_mv[:, t, 0:1], g_tmp[:, 3, t:t + 1],
                                            ALU.subtract, ALU.mult)
                chain_g(ins)
                dve.tensor_scalar(g_h, g_h, 0.0, None, ALU.max)
                dve.tensor_copy(g_a2, g_a12[:, 1:2].broadcast_to([P, P])).then_inc(g_hn, 1)
                for b in range(NB):
                    dve.wait_ge(g_turned, b + 1)
                    dve.tensor_copy(g_ht, ps_t[:, 0]).then_inc(g_t_ok, 1)
                    dve.wait_ge(g_f, b + 1)
                    chain_g(dve.tensor_copy(g_f2[:, 512 * b:512 * (b + 1)], ps_t[:, 1]))
                chain_g(dve.tensor_copy(g_f1, ps_f[:, 0:T]))

                with dve.Fori(0, T) as t:
                    one = bass.ds(t, 1)
                    g_softmax(t, t)
                    g_product(t)
                    after(dve, g_sq, t + 1)
                    chain_g(dve.tensor_scalar(g_rs[:, one], g_s[:, 4:5], 0.5, None, ALU.mult))
                    chain_g(dve.tensor_scalar(g_s[:, 8:9], g_rs[:, one], -1.0, one_less, ALU.mult, ALU.add))
                    chain_g(dve.scalar_tensor_tensor(out=g_feat[:, one, :], in0=g_h[:, one, :], scalar=g_s[:, 8:9],
                                                     in1=ps_s[:, None, 0:F], op0=ALU.mult, op1=ALU.add))
                    chain_g(dve.tensor_scalar(g_wt[:, 0:F], g_feat[:, one, :].rearrange("p o f -> p (o f)"), THRESH, -THRESH,
                                              ALU.min, ALU.max))
                    chain_g(dve.tensor_tensor(g_feat[:, one, :], g_feat[:, one, :], g_wt[:, None, 0:F], ALU.subtract))

                with dve.Fori(0, T) as t:
                    one = bass.ds(t, 1)
                    g_softmax(T + t, t)
                    g_product(T + t)
                    after(dve, g_sq, T + t + 1)
                    pu, odd = ps_s[:, None, 0:F], g_wt[:, None, 0:F]
                    chain_g(dve.scalar_tensor_tensor(out=g_x[:, one, :], in0=g_h0[:, one, :], scalar=h0_share,
                                                     in1=g_x[:, one, :], op0=ALU.mult, op1=ALU.add))
                    chain_g(dve.scalar_tensor_tensor(out=odd, in0=pu, scalar=minus_c3, in1=g_feat[:, one, :],
                                                     op0=ALU.mult, op1=ALU.add))
                    chain_g(dve.scalar_tensor_tensor(out=g_x[:, one, :], in0=pu, scalar=coe[:, 1:2], in1=g_x[:, one, :],
                                                     op0=ALU.mult, op1=ALU.add))
                    chain_g(dve.tensor_scalar(g_s[:, 8:9], g_rs[:, one], coe[:, 1:2], c0_rest, ALU.mult, ALU.add))
                    chain_g(dve.scalar_tensor_tensor(out=g_x[:, one, :], in0=odd, scalar=g_s[:, 8:9], in1=g_x[:, one, :],
                                                     op0=ALU.mult, op1=ALU.add))
                    chain_g(dve.tensor_copy(g_ht[:, 0:F], g_x[:, one, :].rearrange("p o f -> p (o f)")))
                    chain_g(dve.bn_stats(g_st[:, 0, :], g_ht[:, 0:F]))
                    chain_g(dve.bn_aggr(g_mv[:, 0, :], g_st[:, 0, :]))
                    dve.tensor_scalar(g_s[:, 6:7], g_mv[:, 0, 1:2], EPS, None, ALU.add).then_inc(g_var, 1)
                    after(dve, g_root, t + 2)
                    root_refined(g_s[:, 6:7], g_s[:, 7:8], g_s[:, 8:9], g_s[:, 9:10])
                    chain_g(dve.tensor_scalar(g_ht[:, 0:F], g_ht[:, 0:F], g_mv[:, 0, 0:1], g_s[:, 9:10],
                                              ALU.subtract, ALU.mult))
                    dve.tensor_scalar(g_ht[:, 0:F], g_ht[:, 0:F], 0.0, None, ALU.max).then_inc(g_hn, 1)
                    after(dve, g_turned, NB + t + 1)
                    dve.tensor_copy(g_ht[:, P:2 * P], ps_f[:, 0:P]).then_inc(g_t_ok, 1)
                    after(dve, g_f, NB + t + 1)
                    chain_g(dve.tensor_tensor(g_msg[:, one, :], ps_t[:, 1, 0:F][:, None, :], g_bm[:, None, :], ALU.add))

                with dve.Fori(0, T) as t:
                    one = bass.ds(t, 1)
                    n = 2 * T + t
                    after(dve, g_adj_in, 16 * (n + 1))
                    chain_g(dve.tensor_tensor(g_t, g_adj, g_adj, ALU.mult))
                    chain_g(dve.tensor_scalar(g_t, g_t, 1e-4, 0.02, ALU.is_lt, ALU.mult))
                    chain_g(dve.tensor_tensor(g_w, g_t, g_adj, ALU.add))
                    dve.reciprocal(g_w, g_w).then_inc(g_scored, 1)
                    after(dve, g_exp, n + 1)
                    dve.scalar_tensor_tensor(out=g_w, in0=g_adj, scalar=1.0, in1=g_w, op0=ALU.is_lt,
                                             op1=ALU.mult).then_inc(g_w_ok, 1)
                    g_product(n)
                    chain_g(dve.tensor_tensor(g_x[:, one, :], ps_s[:, None, 0:F], g_x[:, one, :], ALU.add))
                dve.sem_inc(g_done, 1)


_INS = ['x', 'adj', 'L0_gnn_h0', 'L0_gnn_a', 'L0_gnn_temp', 'L1_gnn_W', 'L1_gnn_B']


def kernel(**inputs):
    import numpy as _np
    import concourse.bacc as _bacc
    from concourse import mybir as _mybir
    from concourse.bass_utils import run_bass_kernel_spmd as _run

    nc = _bacc.Bacc("TRN2", target_bir_lowering=False, num_devices=1)
    arrays, args = {}, []
    for name in _INS:
        a = _np.ascontiguousarray(inputs[name])
        arrays[f"in_{name}_dram"] = a
        args.append(nc.dram_tensor(f"in_{name}_dram", a.shape, _mybir.dt.from_np(a.dtype), kind="ExternalInput").ap())
    out = nc.dram_tensor("out_dram", (4096, 128), _mybir.dt.float32, kind="ExternalOutput").ap()
    build(nc, *args, out)
    r = _run(nc, [arrays], core_ids=[0])
    return r.results[0]["out_dram"]
```
